# Optimizing a Trainium2 kernel written in Bass

```python
import numpy as np
import jax
import jax.numpy as jnp

def _softmax(x, axis=-1):
    return jax.nn.softmax(x, axis=axis)

def _gelu(x):
    return jax.nn.gelu(x, approximate=True)

def _silu(x):
    return jax.nn.silu(x)

def _sigmoid(x):
    return jax.nn.sigmoid(x)

def _layernorm(x, axis=-1, eps=1e-05):
    m = jnp.mean(x, axis=axis, keepdims=True)
    v = jnp.var(x, axis=axis, keepdims=True)
    return (x - m) / jnp.sqrt(v + eps)

def _scatter_add(tgt, idx, src, axis=0):
    return tgt.at[idx].add(src)

def _segment_sum(src, seg, n):
    return jax.ops.segment_sum(src, seg, n)
kernel_name = 'mk_adj_preln_d1_adj_r2_3d62bc'

def setup_inputs(seed: int=0):
    np.random.seed(seed)
    _w = jnp.asarray

    def _rec_inputs():
        import jax
        import jax.numpy as jnp
        _gk = jax.random.key(seed)
        x = 7.22e-05 + 1 * jax.random.normal(jax.random.fold_in(_gk, 1), (64, 128, 128), jnp.float32)
        _a = jax.random.bernoulli(jax.random.fold_in(_gk, 2), 0.03125, (64, 128, 128))
        _a = jnp.logical_or(_a, jnp.swapaxes(_a, -1, -2))
        _a = jnp.logical_or(_a, jnp.eye(128, dtype=bool))
        _af = _a.astype(jnp.float32)
        adj = _af
        _nm = jnp.ones((64, 128), dtype=bool)
        nodemask = jnp.where(_nm, 1.0, 0.0).astype(jnp.float32)
        return (x, adj, nodemask)
    x, adj, nodemask = _rec_inputs()

    def _L0_gnn_setup():
        import jax, jax.numpy as jnp
        import numpy as np
        B, N, D, C, L = (64, 256, 128, 128, 5)
        EDGE_P = 0.02

        def _gru_cell(m, h, w_ih, w_hh, b_ih, b_hh):
            gi = m @ w_ih.T + b_ih
            gh = h @ w_hh.T + b_hh
            i_r, i_z, i_n = jnp.split(gi, 3, axis=-1)
            h_r, h_z, h_n = jnp.split(gh, 3, axis=-1)
            r = jax.nn.sigmoid(i_r + h_r)
            z = jax.nn.sigmoid(i_z + h_z)
            n = jnp.tanh(i_n + r * h_n)
            return (1.0 - z) * n + z * h
        key = jax.random.key(seed)
        ks = jax.random.split(key, 8)
        x = jax.random.normal(ks[0], (B, N, D), dtype=jnp.float32)
        adj = (jax.random.uniform(ks[1], (B, N, N)) < EDGE_P).astype(jnp.float32)
        mask = jnp.ones((B, N), dtype=jnp.float32)
        s = 1.0 / np.sqrt(C).astype(np.float32)
        weight = jax.random.uniform(ks[2], (L, C, C), minval=-s, maxval=s, dtype=jnp.float32)
        w_ih = jax.random.uniform(ks[3], (3 * C, C), minval=-s, maxval=s, dtype=jnp.float32)
        w_hh = jax.random.uniform(ks[4], (3 * C, C), minval=-s, maxval=s, dtype=jnp.float32)
        b_ih = jax.random.uniform(ks[5], (3 * C,), minval=-s, maxval=s, dtype=jnp.float32)
        b_hh = jax.random.uniform(ks[6], (3 * C,), minval=-s, maxval=s, dtype=jnp.float32)
        return dict(x=x, adj=adj, mask=mask, weight=weight, w_ih=w_ih, w_hh=w_hh, b_ih=b_ih, b_hh=b_hh)
    _L0_gnn_all = _L0_gnn_setup()
    _L0_gnn_in = {k: v for k, v in _L0_gnn_all.items() if k in ('weight', 'w_ih', 'w_hh', 'b_ih', 'b_hh')}
    del _L0_gnn_all
    return {'x': x, 'adj': adj, 'nodemask': nodemask, 'L0_gnn_weight': _L0_gnn_in['weight'], 'L0_gnn_w_ih': _L0_gnn_in['w_ih'], 'L0_gnn_w_hh': _L0_gnn_in['w_hh'], 'L0_gnn_b_ih': _L0_gnn_in['b_ih'], 'L0_gnn_b_hh': _L0_gnn_in['b_hh']}

def reference(x, adj, nodemask, L0_gnn_weight, L0_gnn_w_ih, L0_gnn_w_hh, L0_gnn_b_ih, L0_gnn_b_hh):
    import jax
    import jax.numpy as jnp

    def _L0_gnn_ref(x, adj, mask, weight, w_ih, w_hh, b_ih, b_hh):
        import jax, jax.numpy as jnp
        import numpy as np
        B, N, D, C, L = (64, 256, 128, 128, 5)
        EDGE_P = 0.02

        def _gru_cell(m, h, w_ih, w_hh, b_ih, b_hh):
            gi = m @ w_ih.T + b_ih
            gh = h @ w_hh.T + b_hh
            i_r, i_z, i_n = jnp.split(gi, 3, axis=-1)
            h_r, h_z, h_n = jnp.split(gh, 3, axis=-1)
            r = jax.nn.sigmoid(i_r + h_r)
            z = jax.nn.sigmoid(i_z + h_z)
            n = jnp.tanh(i_n + r * h_n)
            return (1.0 - z) * n + z * h
        A = (adj != 0).astype(x.dtype)
        h = x
        for l in range(weight.shape[0]):
            m = jnp.einsum('bnd,de->bne', h, weight[l])
            agg = jnp.einsum('bij,bid->bjd', A, m)
            h = _gru_cell(agg, h, w_ih, w_hh, b_ih, b_hh)
        return h * mask[..., None]
    h = jnp.maximum(_layernorm(x, axis=-1), 0.0)
    x = x + _L0_gnn_ref(h, adj, nodemask, L0_gnn_weight, L0_gnn_w_ih, L0_gnn_w_hh, L0_gnn_b_ih, L0_gnn_b_hh)
    return x

_drawn_inputs = setup_inputs


def setup_inputs(seed=0):
    import zlib

    import numpy as np

    out = dict(_drawn_inputs(seed))
    spreads = {}
    factors = {}
    for name, (base, spread) in spreads.items():
        noise = np.random.default_rng([zlib.crc32(name.encode()), seed]).standard_normal(out[name].shape)
        drawn = base * np.exp(spread * noise) if base else spread * noise
        out[name] = jnp.asarray(drawn.astype(out[name].dtype))
    for name, factor in factors.items():
        out[name] = (out[name] * factor).astype(out[name].dtype)
    return out
```

```python
from contextlib import ExitStack

import concourse.bass as bass
from concourse import mybir

ALU = mybir.AluOpType
ACT = mybir.ActivationFunctionType
F32 = mybir.dt.float32
F32R = mybir.dt.float32r
F16 = mybir.dt.float16

P = 128
GRAPHS = 4
COLS = GRAPHS * P
SLOTS = 4
GATES = 3
EPS = 1e-5
NAT_SCALE = 2.0 ** 11
DMA = 16

FIRST, MIDDLE, LAST = range(3)


def gnn_kernel(nc, x, adj, mask, weight_t, w_ih_t, w_hh_t, b_ih, b_hh, out):
    B, L = x.shape[0], weight_t.shape[1]
    GROUPS = B // GRAPHS
    WAVES = GROUPS // SLOTS
    ITEMS = L * SLOTS
    V = 2 * GATES * P
    KEPT = (L - 1) * SLOTS
    assert x.shape[1] == P and x.shape[2] == P and GROUPS % SLOTS == 0 and L >= 3 and WAVES >= 2

    x_g = x.rearrange("(g b) n d -> g n b d", b=GRAPHS)
    adj_g = adj.rearrange("(g b) i j -> g i b j", b=GRAPHS)
    out_g = out.rearrange("(g b) n d -> g n b d", b=GRAPHS)

    with ExitStack() as ctx:
        def sb(name, shape, dt=F32):
            return ctx.enter_context(nc.sbuf_tensor(name, shape, dt))

        def bank(name):
            return ctx.enter_context(nc.psum_tensor(name, [P, COLS], F32))

        def sem(name):
            return ctx.enter_context(nc.semaphore(name))

        wt = sb("wt", [P, L, P])
        wih = sb("wih", [P, GATES * P])
        whh = sb("whh", [P, GATES * P])
        whh_hl = sb("whh_hl", [P, V], F32R)
        v_all = sb("v_all", [P, L * V], F32R)
        v_cur = sb("v_cur", [P, V], F32R)
        bih = sb("bih", [P, GATES])
        bhh = sb("bhh", [P, GATES])
        bsum = sb("bsum", [P, GATES])
        ident = sb("ident", [P, P])
        minus_half = sb("minus_half", [P, GRAPHS])
        table_in, table_out = sb("table_in", [P, 1]), sb("table_out", [P, 1])

        x_in = [sb(f"x_in{s}", [P, GRAPHS, P]) for s in range(SLOTS)]
        x_res = [sb(f"x_res{s}", [P, GRAPHS, P]) for s in range(SLOTS)]
        mask_s = [sb(f"mask{s}", [P, GRAPHS]) for s in range(SLOTS)]
        adj_in = [sb(f"adj_in{s}", [P, COLS]) for s in range(SLOTS)]
        edges = [sb(f"edges{s}", [P, COLS], F16) for s in range(SLOTS)]
        hT = [sb(f"hT{s}", [P, COLS]) for s in range(SLOTS)]
        hT_hi = [sb(f"hT_hi{s}", [P, COLS], F32R) for s in range(SLOTS)]
        hT_lo = [sb(f"hT_lo{s}", [P, COLS], F32R) for s in range(SLOTS)]
        y = [sb(f"y{s}", [P, GRAPHS, P]) for s in range(SLOTS)]

        def pair(name, dt=F32):
            return [sb(f"{name}{i}", [P, COLS], dt) for i in range(2)]

        nat_hi, nat_lo = pair("nat_hi", F16), pair("nat_lo", F16)
        agg_hi, agg_lo = pair("agg_hi", F32R), pair("agg_lo", F32R)
        r_sb, z_sb, t_sb, n_sb, d_sb = pair("r"), pair("z"), pair("t"), pair("n"), pair("d")
        h0 = pair("h0")

        centred = [sb(f"centred{s}", [P, GRAPHS, P]) for s in range(SLOTS)]
        mean = [sb(f"mean{s}", [P, GRAPHS]) for s in range(SLOTS)]
        rstd = [sb(f"rstd{s}", [P, GRAPHS]) for s in range(SLOTS)]
        stats = sb("stats", [P, GRAPHS, 6])
        var_eps = [sb(f"var_eps{s}", [P, GRAPHS]) for s in range(SLOTS)]
        spread, var_sum = sb("spread", [P, GRAPHS]), sb("var_sum", [P, GRAPHS])

        ps_t, ps_agg, ps_out = bank("ps_t"), bank("ps_agg"), bank("ps_out")
        ps_r = [bank("ps_r0"), bank("ps_r1")]
        ps_z, ps_hn, ps_in = bank("ps_z"), bank("ps_hn"), bank("ps_in")
        ps_v = [ps_in, ps_hn, ps_z, ps_r[1], ps_out]

        w_loaded, wih_loaded, whh_loaded, b_loaded = sem("w_loaded"), sem("wih_loaded"), sem("whh_loaded"), sem("b_loaded")
        x_loaded = [sem(f"x_loaded{s}") for s in range(SLOTS)]
        adj_loaded = [sem(f"adj_loaded{s}") for s in range(SLOTS)]
        res_loaded = [sem(f"res_loaded{s}") for s in range(SLOTS)]
        stored = [sem(f"stored{s}") for s in range(SLOTS)]
        zeroed, ident_ready, bias_ready = sem("zeroed"), sem("ident_ready"), sem("bias_ready")
        whh_hi_ready, whh_lo_ready = sem("whh_hi_ready"), sem("whh_lo_ready")
        v_done, v_hi_ready, v_lo_ready = sem("v_done"), sem("v_hi_ready"), sem("v_lo_ready")
        t_done, agg_done = sem("t_done"), sem("agg_done")
        r_done, z_done, hn_done, in_done = sem("r_done"), sem("z_done"), sem("hn_done"), sem("in_done")
        nat_hi_ready, nat_lo_ready = sem("nat_hi_ready"), sem("nat_lo_ready")
        agg_hi_ready, agg_lo_ready = sem("agg_hi_ready"), sem("agg_lo_ready")
        r_ready, z_ready, n_ready = sem("r_ready"), sem("z_ready"), sem("n_ready")
        rhn_ready, pre_n_ready = sem("rhn_ready"), sem("pre_n_ready")
        diff_ready, zdiff_ready, h_ready = sem("diff_ready"), sem("zdiff_ready"), sem("h_ready")
        h_hi_ready, h_lo_ready = sem("h_hi_ready"), sem("h_lo_ready")
        v_cur_ready = sem("v_cur_ready")
        stats_ready, mean_ready, var_ready, rstd_ready = sem("stats_ready"), sem("mean_ready"), sem("var_ready"), sem("rstd_ready")
        centred_ready, h0_ready, edges_ready = sem("centred_ready"), sem("h0_ready"), sem("edges_ready")
        h0T_hi_ready, h0T_lo_ready = sem("h0T_hi_ready"), sem("h0T_lo_ready")
        out_done, y_ready = sem("out_done"), sem("y_ready")

        def graph(t, b):
            return t[:, b * P:(b + 1) * P]

        def v_part(layer, part):
            return v_all[:, layer * V + part * V // 2:layer * V + (part + 1) * V // 2]

        def graphs(t):
            return t.rearrange("p (b c) -> p b c", b=GRAPHS)

        def item(w, layer, s):
            return w * ITEMS + layer * SLOTS + s

        def keeps(kind, s):
            return {FIRST: s >= 2, MIDDLE: True, LAST: s < 2}[kind]

        def kept(w, layer, s):
            return w * KEPT + layer * SLOTS + s

        def layers(eng, body):
            def rest(w, after):
                with eng.Fori(1, L - 1) as layer:
                    body(MIDDLE, w, layer, True, True)
                body(LAST, w, L - 1, True, after)

            body(FIRST, 0, 0, False, True)
            with eng.Fori(0, WAVES - 1) as w:
                rest(w, True)
                body(FIRST, w + 1, 0, True, True)
            rest(WAVES - 1, False)

        def finished(kind, w, s, ago):
            if kind == LAST and s >= ago:
                return w, s - ago
            if kind == FIRST and s < ago and not (isinstance(w, int) and w == 0):
                return w - 1, s + SLOTS - ago
            return None

        def entering(kind, w, s, after, ahead):
            if kind == FIRST and s + ahead < SLOTS:
                return w, s + ahead
            if kind == LAST and after and 0 <= s + ahead - SLOTS < SLOTS:
                return w + 1, s + ahead - SLOTS
            return None

        def takes_x(kind, s, after):
            return (kind == FIRST and s < SLOTS - 1) or (kind == LAST and s == SLOTS - 1 and after)

        block = ctx.enter_context(nc.Block())

        @block.sync
        def _(sp):
            def load(w, s):
                g = w * SLOTS + s
                sp.dma_start(x_in[s][:, :, :], x_g[g]).then_inc(x_loaded[s], DMA)
                sp.dma_start(graphs(adj_in[s][:, :]), adj_g[g]).then_inc(adj_loaded[s], DMA)

            def wave(w, before, after):
                for s in range(SLOTS):
                    g = w * SLOTS + s
                    if before:
                        sp.wait_ge(y_ready, (w - 1) * SLOTS + s + 1)
                    sp.wait_ge(x_loaded[s], (w + 1) * DMA)
                    sp.dma_start(x_res[s][:, :, :], x_in[s][:, :, :]).then_inc(res_loaded[s], DMA)
                    sp.dma_start(mask_s[s][:, :], mask[g]).then_inc(res_loaded[s], DMA)
                    if after:
                        sp.wait_ge(centred_ready, w * SLOTS + s + 1)
                        sp.wait_ge(edges_ready, w * SLOTS + s + 1)
                        sp.wait_ge(res_loaded[s], (w + 1) * 2 * DMA)
                        load(w + 1, s)
                for s in range(SLOTS):
                    sp.wait_ge(y_ready, w * SLOTS + s + 1)
                    sp.dma_start(out_g[w * SLOTS + s], y[s][:, :, :]).then_inc(stored[s], DMA)

            for s in range(SLOTS):
                load(0, s)
            wave(0, False, True)
            with sp.Fori(1, WAVES - 1) as w:
                wave(w, True, True)
            wave(WAVES - 1, True, False)
            for s in range(SLOTS):
                sp.wait_ge(stored[s], WAVES * DMA)

        @block.tensor
        def _(pe):
            def aggregate(k, s):
                pe.wait_ge(nat_lo_ready, k + 1)
                for b in range(GRAPHS):
                    for part, nat in enumerate((nat_hi[s % 2], nat_lo[s % 2])):
                        last = nc.tensor.matmul(graph(ps_agg, b), graph(nat, b), graph(edges[s], b),
                                                start=(part == 0), stop=(part == 1))
                last.then_inc(agg_done, 1)

            def product(ps, gate, w_hl, hi, lo, start, stop):
                hi_cols, lo_cols = (slice(at, at + P) for at in (gate * P, (GATES + gate) * P))
                nc.tensor.matmul(ps[:, :], w_hl[:, hi_cols], hi[:, :], start=start, stop=False)
                nc.tensor.matmul(ps[:, :], w_hl[:, lo_cols], hi[:, :], start=False, stop=False)
                return nc.tensor.matmul(ps[:, :], w_hl[:, hi_cols], lo[:, :], start=False, stop=stop)

            def output(w, s, k_last):
                pe.wait_ge(h_ready, k_last + 1)
                if not (isinstance(w, int) and w == 0 and s == 0):
                    pe.wait_ge(y_ready, w * SLOTS + s)
                for b in range(GRAPHS):
                    last = nc.tensor.transpose(graph(ps_out, b), graph(hT[s], b), ident[:, :])
                last.then_inc(out_done, 1)

            def body(kind, w, layer, before, after):
                for s in range(SLOTS):
                    k = item(w, layer, s)
                    nxt = (s + 1) % SLOTS
                    has_next = after or s < SLOTS - 1
                    if has_next:
                        if takes_x(kind, s, after):
                            gw, gs = entering(kind, w, s, after, 1)
                            pe.wait_ge(h0_ready, gw * SLOTS + gs + 1)
                        src = h0[nxt % 2] if takes_x(kind, s, after) else hT[nxt]
                        if not takes_x(kind, s, after):
                            pe.wait_ge(h_ready, k - SLOTS + 2)
                        pe.wait_ge(nat_lo_ready, k + 1)
                        if kind == FIRST:
                            pe.wait_ge(h0T_hi_ready, w * SLOTS + s + 1)
                        for b in range(GRAPHS):
                            last = nc.tensor.transpose(graph(ps_t, b), graph(src, b), ident[:, :])
                        last.then_inc(t_done, 1)

                    if kind == FIRST:
                        pe.wait_ge(h0T_lo_ready, w * SLOTS + s + 1)
                        if not before and s == 0:
                            pe.wait_ge(whh_lo_ready, 1)
                            pe.wait_ge(v_lo_ready, L)
                    else:
                        pe.wait_ge(h_lo_ready, kept(w, layer - 1, s + 1))
                    if before or s >= 2:
                        pe.wait_ge(r_ready, k - 1)
                    product(ps_r[s % 2], 0, whh_hl, hT_hi[s], hT_lo[s], True, False)
                    if before or s >= 1:
                        pe.wait_ge(z_ready, k)
                    product(ps_z, 1, whh_hl, hT_hi[s], hT_lo[s], True, False)
                    if before or s >= 1:
                        pe.wait_ge(rhn_ready, k)
                    product(ps_hn, 2, whh_hl, hT_hi[s], hT_lo[s], True, True).then_inc(hn_done, 1)

                    if has_next:
                        if takes_x(kind, s, after):
                            gw, gs = entering(kind, w, s, after, 1)
                            pe.wait_ge(edges_ready, gw * SLOTS + gs + 1)
                        pe.wait_ge(agg_lo_ready, k + 1)
                        aggregate(k + 1, nxt)
                    else:
                        pe.wait_ge(agg_lo_ready, k + 1)

                    if s == 0:
                        pe.wait_ge(v_cur_ready, w * L + layer + 1)
                    ah, al = agg_hi[s % 2], agg_lo[s % 2]
                    product(ps_r[s % 2], 0, v_cur, ah, al, False, True).then_inc(r_done, 1)
                    product(ps_z, 1, v_cur, ah, al, False, True).then_inc(z_done, 1)
                    if before or s >= 1:
                        pe.wait_ge(pre_n_ready, k)
                    product(ps_in, 2, v_cur, ah, al, True, True).then_inc(in_done, 1)

                    group = finished(kind, w, s, 2)
                    if group:
                        output(*group, k - 2)

            def v_product(layer):
                nc.tensor.matmul(ps_v[layer][:, 0:GATES * P], wt[:, layer, :], wih[:, :],
                                 start=True, stop=True).then_inc(v_done, 1)

            pe.wait_ge(w_loaded, DMA)
            pe.wait_ge(wih_loaded, DMA)
            v_product(0)
            pe.wait_ge(ident_ready, 1)
            pe.wait_ge(h0_ready, 1)
            for b in range(GRAPHS):
                last = nc.tensor.transpose(graph(ps_t, b), graph(h0[0], b), ident[:, :])
            last.then_inc(t_done, 1)
            for layer in range(1, L - 1):
                v_product(layer)
            pe.wait_ge(edges_ready, 1)
            aggregate(0, 0)
            v_product(L - 1)

            layers(pe, body)
            for s in (SLOTS - 2, SLOTS - 1):
                output(WAVES - 1, s, item(WAVES - 1, L - 1, s))

        @block.scalar
        def _(act):
            def relu(w, s):
                g = w * SLOTS + s
                act.wait_ge(rstd_ready, g + 1)
                act.wait_ge(centred_ready, g + 1)
                if not (isinstance(w, int) and w == 0 and s < 2):
                    act.wait_ge(h0T_hi_ready, g - 1)
                    act.wait_ge(nat_lo_ready, item(w, 0, s) - 1 if s >= 2 else item(w - 1, 0, s + 2) + 1)
                for b in range(GRAPHS):
                    last = nc.scalar.activation(graph(h0[s % 2], b), centred[s][:, b, :], ACT.Relu,
                                                scale=rstd[s][:, b:b + 1])
                last.then_inc(h0_ready, 1)

            def nat_high(k, s, src):
                nc.scalar.mul(nat_hi[s % 2][:, :], src[:, :], NAT_SCALE).then_inc(nat_hi_ready, 1)

            def take_h0(w, k, s):
                act.wait_ge(t_done, k + 1)
                if not (isinstance(w, int) and w == 0):
                    act.wait_ge(out_done, (w - 1) * SLOTS + s + 1)
                nc.scalar.copy(hT[s][:, :], ps_t[:, :])
                nc.scalar.copy(hT_hi[s][:, :], ps_t[:, :]).then_inc(h0T_hi_ready, 1)

            def agg_high(k, s, free):
                act.wait_ge(agg_done, k + 1)
                if free:
                    act.wait_ge(in_done, k - 1)
                nc.scalar.copy(agg_hi[s % 2][:, :], ps_agg[:, :]).then_inc(agg_hi_ready, 1)

            def tanh(k, s, free):
                act.wait_ge(pre_n_ready, k + 1)
                if free:
                    act.wait_ge(h_ready, k - 1)
                nc.scalar.activation(n_sb[s % 2][:, :], t_sb[s % 2][:, :], ACT.Tanh,
                                     bias=bih[:, 2:3]).then_inc(n_ready, 1)

            def body(kind, w, layer, before, after):
                for s in range(SLOTS):
                    k = item(w, layer, s)
                    nxt, prv, ago2 = (s + 1) % SLOTS, (s - 1) % SLOTS, (s - 2) % SLOTS
                    has_prev, has_next = before or s > 0, after or s < SLOTS - 1
                    if has_next and takes_x(kind, s, after):
                        gw, gs = entering(kind, w, s, after, 1)
                        act.wait_ge(h0_ready, gw * SLOTS + gs + 1)
                        act.wait_ge(agg_done, k)
                        nat_high(k + 1, gs, h0[gs % 2])
                        take_h0(gw, k + 1, gs)
                    elif has_next:
                        act.wait_ge(t_done, k + 2)
                        act.wait_ge(agg_done, k)
                        nat_high(k + 1, nxt, ps_t)
                    if has_prev:
                        tanh(k - 1, prv, before or s >= 3)
                    if keeps(kind, s):
                        act.wait_ge(h_ready, k - 1)
                        nc.scalar.copy(hT_hi[ago2][:, :], hT[ago2][:, :]).then_inc(h_hi_ready, 1)
                    group = entering(kind, w, s, after, 2)
                    if group:
                        relu(*group)
                    if has_next:
                        agg_high(k + 1, nxt, has_prev)
                    act.wait_ge(r_done, k + 1)
                    if before or s >= 2:
                        act.wait_ge(rhn_ready, k - 1)
                    nc.scalar.activation(r_sb[s % 2][:, :], ps_r[s % 2][:, :], ACT.Sigmoid,
                                         bias=bsum[:, 0:1]).then_inc(r_ready, 1)
                    act.wait_ge(z_done, k + 1)
                    if before or s >= 2:
                        act.wait_ge(zdiff_ready, k - 1)
                    nc.scalar.activation(z_sb[s % 2][:, :], ps_z[:, :], ACT.Sigmoid,
                                         bias=bsum[:, 1:2]).then_inc(z_ready, 1)

            act.dma_start(wih[:, :], w_ih_t).then_inc(wih_loaded, DMA)
            act.dma_start(wt[:, :, :], weight_t).then_inc(w_loaded, DMA)
            act.dma_start(whh[:, :], w_hh_t).then_inc(whh_loaded, DMA)
            act.dma_start(bih[:, :], b_ih).then_inc(b_loaded, DMA)
            act.dma_start(bhh[:, :], b_hh).then_inc(b_loaded, DMA)
            act.wait_ge(zeroed, 1)
            nc.scalar.activation(table_out[:, :], table_in[:, :], ACT.Sigmoid)

            def v_high(layer):
                act.wait_ge(v_done, layer + 1)
                nc.scalar.mul(v_part(layer, 0), ps_v[layer][:, 0:GATES * P], 1 / NAT_SCALE).then_inc(v_hi_ready, 1)

            relu(0, 0)
            act.wait_ge(h0_ready, 1)
            nat_high(0, 0, h0[0])
            act.wait_ge(whh_loaded, DMA)
            nc.scalar.copy(whh_hl[:, 0:V // 2], whh[:, :]).then_inc(whh_hi_ready, 1)
            v_high(0)
            take_h0(0, 0, 0)
            for layer in range(1, L - 1):
                v_high(layer)
            agg_high(0, 0, False)
            v_high(L - 1)
            relu(0, 1)
            act.wait_ge(bias_ready, 1)
            layers(act, body)
            tanh(WAVES * ITEMS - 1, SLOTS - 1, True)

        @block.vector
        def _(dve):
            def edge_matrix(w, s):
                dve.wait_ge(adj_loaded[s], (w + 1) * DMA)
                if not (isinstance(w, int) and w == 0):
                    dve.wait_ge(agg_done, item(w - 1, L - 1, s) + 1)
                nc.vector.tensor_scalar(edges[s][:, :], adj_in[s][:, :], 0.0, None,
                                        ALU.not_equal).then_inc(edges_ready, 1)

            def statistics(w, s):
                g = w * SLOTS + s
                dve.wait_ge(x_loaded[s], (w + 1) * DMA)
                for b in range(GRAPHS):
                    last = nc.vector.bn_stats(stats[:, b, :], x_in[s][:, b, :])
                last.then_inc(stats_ready, 1)
                dve.wait_ge(stats_ready, g + 1)
                nc.vector.tensor_tensor(mean[s][:, :], stats[:, :, 1], stats[:, :, 4], ALU.add)
                nc.vector.tensor_tensor(spread[:, :], stats[:, :, 1], stats[:, :, 4], ALU.subtract)
                nc.vector.tensor_tensor(var_sum[:, :], stats[:, :, 2], stats[:, :, 5], ALU.add).then_inc(mean_ready, 1)
                dve.wait_ge(mean_ready, 3 * g + 1)
                nc.vector.tensor_scalar(mean[s][:, :], mean[s][:, :], 0.5, None, ALU.mult)
                nc.vector.scalar_tensor_tensor(out=spread[:, :], in0=spread[:, :], scalar=P / 4, in1=spread[:, :],
                                               op0=ALU.mult, op1=ALU.mult).then_inc(mean_ready, 1)
                dve.wait_ge(mean_ready, 3 * g + 2)
                nc.vector.tensor_tensor(var_sum[:, :], var_sum[:, :], spread[:, :], ALU.add).then_inc(mean_ready, 1)
                dve.wait_ge(mean_ready, 3 * g + 3)
                nc.vector.tensor_scalar(var_eps[s][:, :], var_sum[:, :], 1.0 / P, EPS, ALU.mult,
                                        ALU.add).then_inc(var_ready, 1)

            def nat_low(k, s, src):
                dve.wait_ge(nat_hi_ready, k + 1)
                nc.vector.scalar_tensor_tensor(out=nat_lo[s % 2][:, :], in0=src[:, :], scalar=NAT_SCALE,
                                               in1=nat_hi[s % 2][:, :], op0=ALU.mult,
                                               op1=ALU.subtract).then_inc(nat_lo_ready, 1)

            def agg_low(k, s, free):
                dve.wait_ge(agg_hi_ready, k + 1)
                if free:
                    dve.wait_ge(in_done, k - 1)
                nc.vector.tensor_tensor(agg_lo[s % 2][:, :], ps_agg[:, :], agg_hi[s % 2][:, :].bitcast(F32),
                                        ALU.subtract).then_inc(agg_lo_ready, 1)

            def pre_n(k, s):
                dve.wait_ge(in_done, k + 1)
                dve.wait_ge(rhn_ready, k + 1)
                nc.vector.tensor_tensor(t_sb[s % 2][:, :], ps_in[:, :], t_sb[s % 2][:, :],
                                        ALU.add).then_inc(pre_n_ready, 1)

            def zdiff(k, s):
                dve.wait_ge(diff_ready, k + 1)
                dve.wait_ge(z_ready, k + 1)
                nc.vector.tensor_tensor(d_sb[s % 2][:, :], z_sb[s % 2][:, :], d_sb[s % 2][:, :],
                                        ALU.mult).then_inc(zdiff_ready, 1)

            def output(w, s):
                g = w * SLOTS + s
                dve.wait_ge(out_done, g + 1)
                dve.wait_ge(res_loaded[s], (w + 1) * 2 * DMA)
                if not (isinstance(w, int) and w == 0):
                    dve.wait_ge(stored[s], w * DMA)
                for b in range(GRAPHS):
                    last = nc.vector.scalar_tensor_tensor(out=y[s][:, b, :], in0=graph(ps_out, b),
                                                          scalar=mask_s[s][:, b:b + 1], in1=x_res[s][:, b, :],
                                                          op0=ALU.mult, op1=ALU.add)
                last.then_inc(y_ready, 1)

            def body(kind, w, layer, before, after):
                for s in range(SLOTS):
                    k = item(w, layer, s)
                    nxt, prv = (s + 1) % SLOTS, (s - 1) % SLOTS
                    has_prev, has_next = before or s > 0, after or s < SLOTS - 1
                    if has_prev:
                        pre_n(k - 1, prv)
                    if takes_x(kind, s, after):
                        nat_low(k + 1, nxt, h0[nxt % 2])
                    elif has_next:
                        nat_low(k + 1, nxt, ps_t)
                    if s == 0:
                        if not before:
                            dve.wait_ge(v_lo_ready, L)
                        nc.vector.tensor_copy(v_cur[:, :], v_all[:, bass.ds(layer * V, V)]).then_inc(v_cur_ready, 1)
                    group = finished(kind, w, s, 3)
                    if group:
                        output(*group)
                    for ahead, job in ((2, edge_matrix), (4, statistics)):
                        group = entering(kind, w, s, after, ahead)
                        if group:
                            job(*group)
                    if has_prev:
                        zdiff(k - 1, prv)
                    if has_next:
                        agg_low(k + 1, nxt, has_prev)
                    dve.wait_ge(r_ready, k + 1)
                    dve.wait_ge(hn_done, k + 1)
                    if before or s >= 2:
                        dve.wait_ge(n_ready, k - 1)
                    nc.vector.scalar_tensor_tensor(out=t_sb[s % 2][:, :], in0=ps_hn[:, :], scalar=bhh[:, 2:3],
                                                   in1=r_sb[s % 2][:, :], op0=ALU.add,
                                                   op1=ALU.mult).then_inc(rhn_ready, 1)

            def v_low(layer):
                dve.wait_ge(v_hi_ready, layer + 1)
                nc.vector.scalar_tensor_tensor(out=v_part(layer, 1), in0=ps_v[layer][:, 0:GATES * P],
                                               scalar=1 / NAT_SCALE, in1=v_part(layer, 0).bitcast(F32),
                                               op0=ALU.mult, op1=ALU.subtract).then_inc(v_lo_ready, 1)

            statistics(0, 0)
            edge_matrix(0, 0)
            statistics(0, 1)
            nat_low(0, 0, h0[0])
            dve.wait_ge(whh_hi_ready, 1)
            nc.vector.tensor_tensor(whh_hl[:, V // 2:V], whh[:, :], whh_hl[:, 0:V // 2].bitcast(F32),
                                    ALU.subtract).then_inc(whh_lo_ready, 1)
            for layer in range(L - 1):
                v_low(layer)
            agg_low(0, 0, False)
            v_low(L - 1)
            dve.wait_ge(b_loaded, 2 * DMA)
            nc.vector.tensor_tensor(bsum[:, :], bih[:, :], bhh[:, :], ALU.add).then_inc(bias_ready, 1)
            edge_matrix(0, 1)
            statistics(0, 2)
            statistics(0, 3)
            layers(dve, body)
            pre_n(WAVES * ITEMS - 1, SLOTS - 1)
            output(WAVES - 1, SLOTS - 3)
            output(WAVES - 1, SLOTS - 2)
            zdiff(WAVES * ITEMS - 1, SLOTS - 1)
            output(WAVES - 1, SLOTS - 1)

        @block.gpsimd
        def _(pool):
            def centre(w, s):
                g = w * SLOTS + s
                pool.wait_ge(var_ready, g + 1)
                nc.gpsimd.tensor_tensor(rstd[s][:, :], var_eps[s][:, :], minus_half[:, :], ALU.pow).then_inc(rstd_ready, 1)
                nc.gpsimd.tensor_tensor(centred[s][:, :, :], x_in[s][:, :, :],
                                        mean[s][:, :].unsqueeze(2).to_broadcast([P, GRAPHS, P]),
                                        ALU.subtract).then_inc(centred_ready, 1)

            def difference(k, s):
                pool.wait_ge(n_ready, k + 1)
                nc.gpsimd.tensor_tensor(d_sb[s % 2][:, :], hT[s][:, :], n_sb[s % 2][:, :],
                                        ALU.subtract).then_inc(diff_ready, 1)

            def update(k, s):
                pool.wait_ge(zdiff_ready, k + 1)
                nc.gpsimd.tensor_tensor(hT[s][:, :], n_sb[s % 2][:, :], d_sb[s % 2][:, :],
                                        ALU.add).then_inc(h_ready, 1)

            def low(s):
                return nc.gpsimd.tensor_tensor(hT_lo[s][:, :], hT[s][:, :], hT_hi[s][:, :].bitcast(F32), ALU.subtract)

            def take_h0(w, s):
                pool.wait_ge(h0T_hi_ready, w * SLOTS + s + 1)
                low(s).then_inc(h0T_lo_ready, 1)

            def body(kind, w, layer, before, after):
                for s in range(SLOTS):
                    k = item(w, layer, s)
                    prv = (s - 1) % SLOTS
                    has_prev = before or s > 0
                    if has_prev:
                        difference(k - 1, prv)
                    if keeps(kind, s):
                        pool.wait_ge(h_hi_ready, kept(w, layer, s) - 1)
                        low((s - 2) % SLOTS).then_inc(h_lo_ready, 1)
                    if takes_x(kind, s, after):
                        take_h0(*entering(kind, w, s, after, 1))
                    if has_prev:
                        update(k - 1, prv)
                    group = entering(kind, w, s, after, 4)
                    if group:
                        centre(*group)

            nc.gpsimd.memset(table_in[:, :], 0.0).then_inc(zeroed, 1)
            nc.gpsimd.memset(ident[:, :], 0.0).then_inc(zeroed, 1)
            pool.wait_ge(zeroed, 2)
            nc.gpsimd.affine_select(out=ident[:, :], in_=ident[:, :], compare_op=ALU.not_equal, fill=1.0, base=0,
                                    pattern=[[-1, P]], channel_multiplier=1).then_inc(ident_ready, 1)
            nc.gpsimd.memset(minus_half[:, :], -0.5).then_inc(zeroed, 1)
            pool.wait_ge(zeroed, 3)
            centre(0, 0)
            centre(0, 1)
            take_h0(0, 0)
            centre(0, 2)
            centre(0, 3)
            layers(pool, body)
            difference(WAVES * ITEMS - 1, SLOTS - 1)
            update(WAVES * ITEMS - 1, SLOTS - 1)


def kernel(x, adj, nodemask, L0_gnn_weight, L0_gnn_w_ih, L0_gnn_w_hh, L0_gnn_b_ih, L0_gnn_b_hh):
    import numpy as np
    import concourse.bacc as bacc
    from concourse.bass_utils import run_bass_kernel_spmd

    lay = np.ascontiguousarray
    x, adj, nodemask = np.asarray(x), np.asarray(adj), np.asarray(nodemask)
    weight, w_ih, w_hh = np.asarray(L0_gnn_weight), np.asarray(L0_gnn_w_ih), np.asarray(L0_gnn_w_hh)
    b_ih, b_hh = np.asarray(L0_gnn_b_ih), np.asarray(L0_gnn_b_hh)
    arrays = {
        "x": lay(x),
        "adj": lay(adj),
        "mask": lay(nodemask.reshape(-1, GRAPHS, P).transpose(0, 2, 1)),
        "weight_t": lay(weight.transpose(2, 0, 1)),
        "w_ih_t": lay(w_ih.T),
        "w_hh_t": lay(w_hh.T),
        "b_ih": lay(b_ih.reshape(GATES, P).T),
        "b_hh": lay(b_hh.reshape(GATES, P).T),
    }
    nc = bacc.Bacc("TRN2", target_bir_lowering=False, num_devices=1)
    args = [nc.dram_tensor(f"in_{n}", a.shape, mybir.dt.from_np(a.dtype), kind="ExternalInput").ap()
            for n, a in arrays.items()]
    out = nc.dram_tensor("out", x.shape, F32, kind="ExternalOutput").ap()
    gnn_kernel(nc, *args, out)
    r = run_bass_kernel_spmd(nc, [{f"in_{n}": a for n, a in arrays.items()}], core_ids=[0])
    return r.results[0]["out"]
```

```python
from contextlib import ExitStack

import concourse.bass as bass
from concourse import mybir

ALU = mybir.AluOpType
ACT = mybir.ActivationFunctionType
F32 = mybir.dt.float32
F32R = mybir.dt.float32r
F16 = mybir.dt.float16

P = 128
GRAPHS = 4
COLS = GRAPHS * P
SLOTS = 4
GATES = 3
EPS = 1e-5
NAT_SCALE = 2.0 ** 11
DMA = 16

FIRST, MIDDLE, LAST = range(3)


def gnn_kernel(nc, x, adj, mask, weight_t, w_ih_t, w_hh_t, b_ih, b_hh, out):
    B, L = x.shape[0], weight_t.shape[1]
    GROUPS = B // GRAPHS
    WAVES = GROUPS // SLOTS
    ITEMS = L * SLOTS
    V = 2 * GATES * P
    KEPT = (L - 1) * SLOTS
    assert L - 1 == SLOTS
    assert x.shape[1] == P and x.shape[2] == P and GROUPS % SLOTS == 0 and L >= 3 and WAVES >= 2

    x_g = x.rearrange("(g b) n d -> g n b d", b=GRAPHS)
    adj_g = adj.rearrange("(g b) i j -> g i b j", b=GRAPHS)
    out_g = out.rearrange("(g b) n d -> g n b d", b=GRAPHS)

    with ExitStack() as ctx:
        def sb(name, shape, dt=F32):
            return ctx.enter_context(nc.sbuf_tensor(name, shape, dt))

        def bank(name):
            return ctx.enter_context(nc.psum_tensor(name, [P, COLS], F32))

        def sem(name):
            return ctx.enter_context(nc.semaphore(name))

        wt = sb("wt", [P, L, P])
        wih = sb("wih", [P, GATES * P])
        whh = sb("whh", [P, GATES * P])
        whh_hl = sb("whh_hl", [P, V], F32R)
        v_all = sb("v_all", [P, L * V], F32R)
        v_cur = sb("v_cur", [P, V], F32R)
        bih = sb("bih", [P, GATES])
        bhh = sb("bhh", [P, GATES])
        bsum = sb("bsum", [P, GATES])
        ident = sb("ident", [P, P])
        minus_half = sb("minus_half", [P, GRAPHS])
        table_in, table_out = sb("table_in", [P, 1]), sb("table_out", [P, 1])

        x_in = sb("x_in", [P, SLOTS * GRAPHS, P])
        x_res = [sb(f"x_res{s}", [P, GRAPHS, P]) for s in range(SLOTS)]
        mask_s = [sb(f"mask{s}", [P, GRAPHS]) for s in range(SLOTS)]
        adj_in = [sb(f"adj_in{s}", [P, COLS]) for s in range(SLOTS)]
        edges = [sb(f"edges{s}", [P, COLS], F16) for s in range(SLOTS)]
        hT = [sb(f"hT{s}", [P, COLS]) for s in range(SLOTS)]
        hT_hi = [sb(f"hT_hi{s}", [P, COLS], F32R) for s in range(SLOTS)]
        hT_lo = [sb(f"hT_lo{s}", [P, COLS], F32R) for s in range(SLOTS)]
        y = [sb(f"y{s}", [P, GRAPHS, P]) for s in range(SLOTS)]

        def each_slot(name, shape):
            return [sb(f"{name}{s}", shape) for s in range(SLOTS)]

        def pair(name, dt=F32):
            return [sb(f"{name}{i}", [P, COLS], dt) for i in range(2)]

        nat_hi, nat_lo = pair("nat_hi", F16), pair("nat_lo", F16)
        agg_hi, agg_lo = pair("agg_hi", F32R), pair("agg_lo", F32R)
        r_sb, z_sb, t_sb, n_sb, d_sb = pair("r"), pair("z"), pair("t"), pair("n"), pair("d")

        normed = sb("normed", [P, SLOTS * COLS])
        stats = each_slot("stats", [P, GRAPHS, 6])
        sums = each_slot("sums", [P, GRAPHS, 2])
        mean, spread, var_part = (each_slot(name, [P, GRAPHS]) for name in ("mean", "spread", "var_part"))
        var_eps = each_slot("var_eps", [P, GRAPHS])
        rstd = each_slot("rstd", [P, GRAPHS])
        ps_t, ps_agg, ps_out = bank("ps_t"), bank("ps_agg"), bank("ps_out")
        ps_r = [bank("ps_r0"), bank("ps_r1")]
        ps_z, ps_hn, ps_in = bank("ps_z"), bank("ps_hn"), bank("ps_in")
        ps_v = [ps_in, ps_hn, ps_z, ps_out, ps_out]
        EARLY_V = 3

        w_loaded, wih_loaded, whh_loaded, b_loaded = sem("w_loaded"), sem("wih_loaded"), sem("whh_loaded"), sem("b_loaded")
        x_loaded = [sem(f"x_loaded{s}") for s in range(SLOTS)]
        adj_loaded = [sem(f"adj_loaded{s}") for s in range(SLOTS)]
        res_loaded = [sem(f"res_loaded{s}") for s in range(SLOTS)]
        stored = [sem(f"stored{s}") for s in range(SLOTS)]
        zeroed, ident_ready, bias_ready = sem("zeroed"), sem("ident_ready"), sem("bias_ready")
        whh_hi_ready, whh_lo_ready = sem("whh_hi_ready"), sem("whh_lo_ready")
        v_done, v_hi_ready, v_lo_ready = sem("v_done"), sem("v_hi_ready"), sem("v_lo_ready")
        t_done, agg_done = sem("t_done"), sem("agg_done")
        r_done, z_done, hn_done, in_done = sem("r_done"), sem("z_done"), sem("hn_done"), sem("in_done")
        nat_hi_ready, nat_lo_ready = sem("nat_hi_ready"), sem("nat_lo_ready")
        agg_hi_ready, agg_lo_ready = sem("agg_hi_ready"), sem("agg_lo_ready")
        r_ready, z_ready, n_ready = sem("r_ready"), sem("z_ready"), sem("n_ready")
        rhn_ready, pre_n_ready = sem("rhn_ready"), sem("pre_n_ready")
        diff_ready, zdiff_ready, h_ready = sem("diff_ready"), sem("zdiff_ready"), sem("h_ready")
        last_diff_ready, last_zdiff_ready, last_h_ready = sem("last_diff_ready"), sem("last_zdiff_ready"), sem("last_h_ready")
        h_hi_ready, h_lo_ready = sem("h_hi_ready"), sem("h_lo_ready")
        v_cur_ready = sem("v_cur_ready")
        stats_ready, sums_ready, squares_ready = sem("stats_ready"), sem("sums_ready"), sem("squares_ready")
        var_ready, rstd_ready = sem("var_ready"), sem("rstd_ready")
        normed_ready, edges_ready = sem("normed_ready"), sem("edges_ready")
        h0T_hi_ready, h0T_lo_ready = sem("h0T_hi_ready"), sem("h0T_lo_ready")
        out_done, y_ready = sem("out_done"), sem("y_ready")

        def graph(t, b):
            return t[:, b * P:(b + 1) * P]

        def v_part(layer, part):
            return v_all[:, layer * V + part * V // 2:layer * V + (part + 1) * V // 2]

        def x_slot(s):
            return x_in[:, s * GRAPHS:(s + 1) * GRAPHS, :]

        def normed_slot(s):
            return normed[:, s * COLS:(s + 1) * COLS]

        def graphs(t):
            return t.rearrange("p (b c) -> p b c", b=GRAPHS)

        def item(w, layer, s):
            return w * ITEMS + layer * SLOTS + s

        def keeps(kind, s):
            return {FIRST: s >= 2, MIDDLE: True, LAST: s < 2}[kind]

        def kept(w, layer, s):
            return w * KEPT + layer * SLOTS + s

        def layers(eng, body):
            def rest(w, after):
                with eng.Fori(1, L - 1) as layer:
                    body(MIDDLE, w, layer, True, after)
                body(LAST, w, L - 1, True, after)

            body(FIRST, 0, 0, False, True)
            with eng.Fori(0, WAVES - 1) as w:
                rest(w, True)
                body(FIRST, w + 1, 0, True, True)
            rest(WAVES - 1, False)

        def finished(kind, w, s, ago):
            if kind == LAST and s >= ago:
                return w, s - ago
            if kind == FIRST and s < ago and not (isinstance(w, int) and w == 0):
                return w - 1, s + SLOTS - ago
            return None

        def entering(kind, w, s, after, ahead):
            if kind == FIRST and s + ahead < SLOTS:
                return w, s + ahead
            if kind == LAST and after and 0 <= s + ahead - SLOTS < SLOTS:
                return w + 1, s + ahead - SLOTS
            return None

        def takes_x(kind, s, after):
            return (kind == FIRST and s < SLOTS - 1) or (kind == LAST and s == SLOTS - 1 and after)

        block = ctx.enter_context(nc.Block())

        @block.sync
        def _(sp):
            def load_x(w, s):
                sp.dma_start(x_slot(s), x_g[w * SLOTS + s]).then_inc(x_loaded[s], DMA)

            def load_adj(w, s):
                sp.dma_start(graphs(adj_in[s][:, :]), adj_g[w * SLOTS + s]).then_inc(adj_loaded[s], DMA)

            def load(w):
                for s in range(SLOTS):
                    sp.wait_ge(normed_ready, (w - 1) * SLOTS + s + 1)
                    sp.wait_ge(edges_ready, (w - 1) * SLOTS + s + 1)
                    sp.wait_ge(res_loaded[s], w * 2 * DMA)
                    load_x(w, s)
                    load_adj(w, s)

            def residual(w, s):
                sp.wait_ge(x_loaded[s], (w + 1) * DMA)
                sp.dma_start(x_res[s][:, :, :], x_slot(s)).then_inc(res_loaded[s], DMA)
                sp.dma_start(mask_s[s][:, :], mask[w * SLOTS + s]).then_inc(res_loaded[s], DMA)

            def wave_end(w, after):
                for s in range(SLOTS):
                    sp.wait_ge(y_ready, w * SLOTS + s + 1)
                    sp.dma_start(out_g[w * SLOTS + s], y[s][:, :, :]).then_inc(stored[s], DMA)
                    if after:
                        residual(w + 1, s)

            for s in range(0, SLOTS, 2):
                for do in (load_x, load_adj):
                    do(0, s)
                    do(0, s + 1)
            for s in range(SLOTS):
                residual(0, s)
            load(1)
            with sp.Fori(0, WAVES - 2) as w:
                wave_end(w, True)
                load(w + 2)
            wave_end(WAVES - 2, True)
            wave_end(WAVES - 1, False)
            for s in range(SLOTS):
                sp.wait_ge(stored[s], WAVES * DMA)

        @block.tensor
        def _(pe):
            def aggregate(k, s):
                pe.wait_ge(nat_lo_ready, k + 1)
                for b in range(GRAPHS):
                    for part, nat in enumerate((nat_hi[s % 2], nat_lo[s % 2])):
                        last = nc.tensor.matmul(graph(ps_agg, b), graph(nat, b), graph(edges[s], b),
                                                start=(part == 0), stop=(part == 1))
                last.then_inc(agg_done, 1)

            def product(ps, gate, w_hl, hi, lo, start, stop):
                hi_cols, lo_cols = (slice(at, at + P) for at in (gate * P, (GATES + gate) * P))
                nc.tensor.matmul(ps[:, :], w_hl[:, hi_cols], hi[:, :], start=start, stop=False)
                nc.tensor.matmul(ps[:, :], w_hl[:, lo_cols], hi[:, :], start=False, stop=False)
                return nc.tensor.matmul(ps[:, :], w_hl[:, hi_cols], lo[:, :], start=False, stop=stop)

            def output(w, s, k_last):
                if k_last is not None:
                    pe.wait_ge(h_ready, k_last + 1)
                if not (isinstance(w, int) and w == 0 and s == 0):
                    pe.wait_ge(y_ready, w * SLOTS + s)
                for b in range(GRAPHS):
                    last = nc.tensor.transpose(graph(ps_out, b), graph(hT[s], b), ident[:, :])
                last.then_inc(out_done, 1)

            def body(kind, w, layer, before, after):
                for s in range(SLOTS):
                    k = item(w, layer, s)
                    nxt = (s + 1) % SLOTS
                    has_next = after or kind != LAST or s < SLOTS - 1
                    if has_next:
                        if takes_x(kind, s, after):
                            gw, gs = entering(kind, w, s, after, 1)
                            pe.wait_ge(normed_ready, gw * SLOTS + gs + 1)
                        src = normed_slot(nxt) if takes_x(kind, s, after) else hT[nxt]
                        if not takes_x(kind, s, after):
                            pe.wait_ge(h_ready, k - SLOTS + 2)
                        pe.wait_ge(nat_lo_ready, k + 1)
                        if kind == FIRST:
                            pe.wait_ge(h0T_hi_ready, w * SLOTS + s + 1)
                        for b in range(GRAPHS):
                            last = nc.tensor.transpose(graph(ps_t, b), graph(src, b), ident[:, :])
                        last.then_inc(t_done, 1)

                    if kind == FIRST:
                        pe.wait_ge(h0T_lo_ready, w * SLOTS + s + 1)
                        if not before and s == 0:
                            pe.wait_ge(whh_lo_ready, 1)
                    else:
                        pe.wait_ge(h_lo_ready, kept(w, layer - 1, s + 1))
                    if before or s >= 2:
                        pe.wait_ge(r_ready, k - 1)
                    product(ps_r[s % 2], 0, whh_hl, hT_hi[s], hT_lo[s], True, False)
                    if before or s >= 1:
                        pe.wait_ge(z_ready, k)
                    else:
                        pe.wait_ge(v_lo_ready, ps_v.index(ps_z) + 1)
                    product(ps_z, 1, whh_hl, hT_hi[s], hT_lo[s], True, False)
                    if before or s >= 1:
                        pe.wait_ge(rhn_ready, k)
                    else:
                        pe.wait_ge(v_lo_ready, ps_v.index(ps_hn) + 1)
                    product(ps_hn, 2, whh_hl, hT_hi[s], hT_lo[s], True, True).then_inc(hn_done, 1)

                    if has_next:
                        if takes_x(kind, s, after):
                            gw, gs = entering(kind, w, s, after, 1)
                            pe.wait_ge(edges_ready, gw * SLOTS + gs + 1)
                        pe.wait_ge(agg_lo_ready, k + 1)
                        aggregate(k + 1, nxt)
                    else:
                        pe.wait_ge(agg_lo_ready, k + 1)

                    if s == 0:
                        pe.wait_ge(v_cur_ready, w * L + layer + 1)
                    ah, al = agg_hi[s % 2], agg_lo[s % 2]
                    product(ps_r[s % 2], 0, v_cur, ah, al, False, True).then_inc(r_done, 1)
                    product(ps_z, 1, v_cur, ah, al, False, True).then_inc(z_done, 1)
                    if before or s >= 1:
                        pe.wait_ge(pre_n_ready, k)
                    product(ps_in, 2, v_cur, ah, al, True, True).then_inc(in_done, 1)

                    if not before and EARLY_V + s < L:
                        if s > 0:
                            pe.wait_ge(v_lo_ready, EARLY_V + s)
                        v_product(EARLY_V + s)
                    group = finished(kind, w, s, 2)
                    if group:
                        output(*group, k - 2)

            def v_product(layer):
                nc.tensor.matmul(ps_v[layer][:, 0:GATES * P], wt[:, layer, :], wih[:, :],
                                 start=True, stop=True).then_inc(v_done, 1)

            pe.wait_ge(w_loaded, DMA)
            pe.wait_ge(wih_loaded, DMA)
            v_product(0)
            pe.wait_ge(ident_ready, 1)
            pe.wait_ge(normed_ready, 1)
            for b in range(GRAPHS):
                last = nc.tensor.transpose(graph(ps_t, b), graph(normed, b), ident[:, :])
            last.then_inc(t_done, 1)
            for layer in range(1, EARLY_V):
                v_product(layer)
            pe.wait_ge(edges_ready, 1)
            aggregate(0, 0)

            layers(pe, body)
            output(WAVES - 1, SLOTS - 2, item(WAVES - 1, L - 1, SLOTS - 2))
            pe.wait_ge(last_h_ready, 1)
            output(WAVES - 1, SLOTS - 1, None)

        @block.scalar
        def _(act):
            def nat_high(k, s, src, function, scale):
                nc.scalar.activation(nat_hi[s % 2][:, :], src, function, scale=scale).then_inc(nat_hi_ready, 1)

            def take_x(w, k, s):
                act.wait_ge(normed_ready, w * SLOTS + s + 1)
                nat_high(k, s, normed_slot(s), ACT.Relu, 1.0)
                act.wait_ge(t_done, k + 1)
                if not (isinstance(w, int) and w == 0):
                    act.wait_ge(out_done, (w - 1) * SLOTS + s + 1)
                nc.scalar.activation(hT[s][:, :], ps_t[:, :], ACT.Relu, scale=1 / NAT_SCALE)
                nc.scalar.activation(hT_hi[s][:, :], ps_t[:, :], ACT.Relu,
                                     scale=1 / NAT_SCALE).then_inc(h0T_hi_ready, 1)

            def agg_high(k, s, free):
                act.wait_ge(agg_done, k + 1)
                if free:
                    act.wait_ge(in_done, k - 1)
                nc.scalar.copy(agg_hi[s % 2][:, :], ps_agg[:, :]).then_inc(agg_hi_ready, 1)

            def tanh(k, s, free):
                act.wait_ge(pre_n_ready, k + 1)
                if free:
                    act.wait_ge(h_ready, k - 1)
                nc.scalar.activation(n_sb[s % 2][:, :], t_sb[s % 2][:, :], ACT.Tanh,
                                     bias=bih[:, 2:3]).then_inc(n_ready, 1)

            def body(kind, w, layer, before, after):
                for s in range(SLOTS):
                    k = item(w, layer, s)
                    nxt, prv, ago2 = (s + 1) % SLOTS, (s - 1) % SLOTS, (s - 2) % SLOTS
                    has_prev, has_next = before or s > 0, after or kind != LAST or s < SLOTS - 1
                    if has_next and takes_x(kind, s, after):
                        gw, gs = entering(kind, w, s, after, 1)
                        act.wait_ge(agg_done, k)
                        take_x(gw, k + 1, gs)
                    elif has_next:
                        act.wait_ge(t_done, k + 2)
                        act.wait_ge(agg_done, k)
                        nat_high(k + 1, nxt, ps_t[:, :], ACT.Copy, NAT_SCALE)
                    if has_prev:
                        tanh(k - 1, prv, before or s >= 3)
                    if keeps(kind, s):
                        act.wait_ge(h_ready, k - 1)
                        nc.scalar.copy(hT_hi[ago2][:, :], hT[ago2][:, :]).then_inc(h_hi_ready, 1)
                    if has_next:
                        agg_high(k + 1, nxt, has_prev)
                    act.wait_ge(r_done, k + 1)
                    if before or s >= 2:
                        act.wait_ge(rhn_ready, k - 1)
                    nc.scalar.activation(r_sb[s % 2][:, :], ps_r[s % 2][:, :], ACT.Sigmoid,
                                         bias=bsum[:, 0:1]).then_inc(r_ready, 1)
                    act.wait_ge(z_done, k + 1)
                    if before or s >= 2:
                        act.wait_ge(zdiff_ready, k - 1)
                    nc.scalar.activation(z_sb[s % 2][:, :], ps_z[:, :], ACT.Sigmoid,
                                         bias=bsum[:, 1:2]).then_inc(z_ready, 1)
                    if not before and EARLY_V + s < L:
                        v_high(EARLY_V + s)

            act.dma_start(wih[:, :], w_ih_t).then_inc(wih_loaded, DMA)
            act.dma_start(wt[:, :, :], weight_t).then_inc(w_loaded, DMA)
            act.dma_start(whh[:, :], w_hh_t).then_inc(whh_loaded, DMA)
            act.dma_start(bih[:, :], b_ih).then_inc(b_loaded, DMA)
            act.dma_start(bhh[:, :], b_hh).then_inc(b_loaded, DMA)
            act.wait_ge(zeroed, 1)
            nc.scalar.activation(table_out[:, :], table_in[:, :], ACT.Sigmoid)

            def v_high(layer):
                act.wait_ge(v_done, layer + 1)
                nc.scalar.mul(v_part(layer, 0), ps_v[layer][:, 0:GATES * P], 1 / NAT_SCALE).then_inc(v_hi_ready, 1)

            act.wait_ge(whh_loaded, DMA)
            nc.scalar.copy(whh_hl[:, 0:V // 2], whh[:, :]).then_inc(whh_hi_ready, 1)
            v_high(0)
            take_x(0, 0, 0)
            for layer in range(1, EARLY_V):
                v_high(layer)
            agg_high(0, 0, False)
            act.wait_ge(bias_ready, 1)
            layers(act, body)
            tanh(WAVES * ITEMS - 1, SLOTS - 1, True)

        @block.vector
        def _(dve):
            def edge_matrix(w, s):
                dve.wait_ge(adj_loaded[s], (w + 1) * DMA)
                if not (isinstance(w, int) and w == 0):
                    dve.wait_ge(agg_done, item(w - 1, L - 1, s) + 1)
                nc.vector.tensor_scalar(edges[s][:, :], adj_in[s][:, :], 0.0, None,
                                        ALU.not_equal).then_inc(edges_ready, 1)

            def statistics(w, s, i):
                for slot in (s,) if isinstance(s, int) else range(SLOTS):
                    dve.wait_ge(x_loaded[slot], (w + 1) * DMA)
                for b in range(GRAPHS):
                    last = nc.vector.bn_stats(stats[i][:, b, :], x_graph(s, b))
                last.then_inc(stats_ready, 1)

            def norm_sums(w, s, i):
                dve.wait_ge(stats_ready, w * SLOTS + s + 1)
                nc.vector.tensor_tensor(sums[i][:, :, :], stats[i][:, :, 1:3], stats[i][:, :, 4:6], ALU.add)
                nc.vector.tensor_tensor(spread[i][:, :], stats[i][:, :, 1], stats[i][:, :, 4],
                                        ALU.subtract).then_inc(sums_ready, 1)

            def norm_squares(w, s, i):
                dve.wait_ge(sums_ready, w * SLOTS + s + 1)
                nc.vector.tensor_scalar(mean[i][:, :], sums[i][:, :, 0], 0.5, None, ALU.mult)
                nc.vector.tensor_scalar(var_part[i][:, :], sums[i][:, :, 1], 1 / P / NAT_SCALE ** 2,
                                        EPS / NAT_SCALE ** 2, ALU.mult, ALU.add)
                nc.vector.scalar_tensor_tensor(out=spread[i][:, :], in0=spread[i][:, :], scalar=0.25 / NAT_SCALE ** 2,
                                               in1=spread[i][:, :], op0=ALU.mult, op1=ALU.mult).then_inc(squares_ready, 1)

            def variance(w, s, i):
                dve.wait_ge(squares_ready, w * SLOTS + s + 1)
                nc.vector.tensor_tensor(var_eps[i][:, :], var_part[i][:, :], spread[i][:, :],
                                        ALU.add).then_inc(var_ready, 1)

            def normalise(w, s, i):
                dve.wait_ge(rstd_ready, w * SLOTS + s + 1)
                for b in range(GRAPHS):
                    last = nc.vector.tensor_scalar(normed[:, bass.ds(s * COLS + b * P, P)], x_graph(s, b),
                                                   mean[i][:, b:b + 1], rstd[i][:, b:b + 1], ALU.subtract, ALU.mult)
                last.then_inc(normed_ready, 1)

            def x_graph(s, b):
                return x_flat[:, bass.ds(s * COLS + b * P, P)]

            x_flat = x_in[:, :, :].rearrange("p g c -> p (g c)")

            def nat_low(k, s, src, op, scalar):
                dve.wait_ge(nat_hi_ready, k + 1)
                nc.vector.scalar_tensor_tensor(out=nat_lo[s % 2][:, :], in0=src, scalar=scalar,
                                               in1=nat_hi[s % 2][:, :], op0=op,
                                               op1=ALU.subtract).then_inc(nat_lo_ready, 1)

            def agg_low(k, s, free):
                dve.wait_ge(agg_hi_ready, k + 1)
                if free:
                    dve.wait_ge(in_done, k - 1)
                nc.vector.tensor_tensor(agg_lo[s % 2][:, :], ps_agg[:, :], agg_hi[s % 2][:, :].bitcast(F32),
                                        ALU.subtract).then_inc(agg_lo_ready, 1)

            def pre_n(k, s):
                dve.wait_ge(in_done, k + 1)
                dve.wait_ge(rhn_ready, k + 1)
                nc.vector.tensor_tensor(t_sb[s % 2][:, :], ps_in[:, :], t_sb[s % 2][:, :],
                                        ALU.add).then_inc(pre_n_ready, 1)

            def zdiff(k, s):
                dve.wait_ge(diff_ready, k + 1)
                dve.wait_ge(z_ready, k + 1)
                nc.vector.tensor_tensor(d_sb[s % 2][:, :], z_sb[s % 2][:, :], d_sb[s % 2][:, :],
                                        ALU.mult).then_inc(zdiff_ready, 1)

            def output(w, s):
                g = w * SLOTS + s
                dve.wait_ge(out_done, g + 1)
                dve.wait_ge(res_loaded[s], (w + 1) * 2 * DMA)
                if not (isinstance(w, int) and w == 0):
                    dve.wait_ge(stored[s], w * DMA)
                for b in range(GRAPHS):
                    last = nc.vector.scalar_tensor_tensor(out=y[s][:, b, :], in0=graph(ps_out, b),
                                                          scalar=mask_s[s][:, b:b + 1], in1=x_res[s][:, b, :],
                                                          op0=ALU.mult, op1=ALU.add)
                last.then_inc(y_ready, 1)

            def body(kind, w, layer, before, after):
                for s in range(SLOTS):
                    k = item(w, layer, s)
                    nxt, prv = (s + 1) % SLOTS, (s - 1) % SLOTS
                    has_prev, has_next = before or s > 0, after or kind != LAST or s < SLOTS - 1
                    if has_prev:
                        pre_n(k - 1, prv)
                    if takes_x(kind, s, after):
                        nat_low(k + 1, nxt, normed_slot(nxt), ALU.max, 0.0)
                    elif has_next:
                        nat_low(k + 1, nxt, ps_t[:, :], ALU.mult, NAT_SCALE)
                    first_steps = not before and s < 2
                    if first_steps and s == 0:
                        norm_sums(0, 3, 3)
                    if s == 0:
                        dve.wait_ge(v_lo_ready, L if before else 1)
                        nc.vector.tensor_copy(v_cur[:, :], v_all[:, bass.ds(layer * V, V)]).then_inc(v_cur_ready, 1)
                    group = finished(kind, w, s, 3)
                    if group:
                        output(*group)
                    if first_steps and s == 0:
                        norm_squares(0, 3, 3)
                    group = entering(kind, w, s, after, 2)
                    if group:
                        edge_matrix(*group)
                    if first_steps and s == 0:
                        variance(0, 3, 3)
                    if first_steps:
                        normalise(0, s + 2, s + 2)
                    group = (w + 1, layer - 1, 0) if kind != FIRST and after else None
                    if group and s == 0:
                        statistics(*group)
                    if group and s == 1:
                        norm_squares(*group)
                        variance(*group)
                    if group and s == 2:
                        normalise(*group)
                    if has_next:
                        agg_low(k + 1, nxt, has_prev)
                    if has_prev:
                        zdiff(k - 1, prv)
                    if group and s == 0:
                        norm_sums(*group)
                    dve.wait_ge(r_ready, k + 1)
                    dve.wait_ge(hn_done, k + 1)
                    if before or s >= 2:
                        dve.wait_ge(n_ready, k - 1)
                    nc.vector.scalar_tensor_tensor(out=t_sb[s % 2][:, :], in0=ps_hn[:, :], scalar=bhh[:, 2:3],
                                                   in1=r_sb[s % 2][:, :], op0=ALU.add,
                                                   op1=ALU.mult).then_inc(rhn_ready, 1)
                    if not before and EARLY_V + s < L:
                        v_low(EARLY_V + s)

            def v_low(layer):
                dve.wait_ge(v_hi_ready, layer + 1)
                nc.vector.scalar_tensor_tensor(out=v_part(layer, 1), in0=ps_v[layer][:, 0:GATES * P],
                                               scalar=1 / NAT_SCALE, in1=v_part(layer, 0).bitcast(F32),
                                               op0=ALU.mult, op1=ALU.subtract).then_inc(v_lo_ready, 1)

            def whh_low():
                dve.wait_ge(whh_hi_ready, 1)
                nc.vector.tensor_tensor(whh_hl[:, V // 2:V], whh[:, :], whh_hl[:, 0:V // 2].bitcast(F32),
                                        ALU.subtract).then_inc(whh_lo_ready, 1)

            def norm(s):
                for step in (statistics, norm_sums, norm_squares, variance):
                    step(0, s, s)

            norm(0)
            norm(1)
            normalise(0, 0, 0)
            edge_matrix(0, 0)
            normalise(0, 1, 1)
            nat_low(0, 0, normed_slot(0), ALU.max, 0.0)
            whh_low()
            for layer in range(EARLY_V - 1):
                v_low(layer)
            statistics(0, 2, 2)
            v_low(EARLY_V - 1)
            edge_matrix(0, 1)
            norm_sums(0, 2, 2)
            agg_low(0, 0, False)
            norm_squares(0, 2, 2)
            dve.wait_ge(b_loaded, 2 * DMA)
            nc.vector.tensor_tensor(bsum[:, :], bih[:, :], bhh[:, :], ALU.add).then_inc(bias_ready, 1)
            variance(0, 2, 2)
            statistics(0, 3, 3)
            layers(dve, body)
            k, s = WAVES * ITEMS - 1, SLOTS - 1
            pre_n(k, s)
            output(WAVES - 1, s - 2)
            dve.wait_ge(n_ready, k + 1)
            nc.vector.tensor_tensor(d_sb[s % 2][:, :], hT[s][:, :], n_sb[s % 2][:, :],
                                    ALU.subtract).then_inc(last_diff_ready, 1)
            dve.wait_ge(last_diff_ready, 1)
            dve.wait_ge(z_ready, k + 1)
            nc.vector.tensor_tensor(d_sb[s % 2][:, :], z_sb[s % 2][:, :], d_sb[s % 2][:, :],
                                    ALU.mult).then_inc(last_zdiff_ready, 1)
            dve.wait_ge(last_zdiff_ready, 1)
            nc.vector.tensor_tensor(hT[s][:, :], n_sb[s % 2][:, :], d_sb[s % 2][:, :],
                                    ALU.add).then_inc(last_h_ready, 1)
            output(WAVES - 1, s - 1)
            output(WAVES - 1, s)

        @block.gpsimd
        def _(pool):
            def root(w, s, i):
                pool.wait_ge(var_ready, w * SLOTS + s + 1)
                nc.gpsimd.tensor_tensor(rstd[i][:, :], var_eps[i][:, :], minus_half[:, :],
                                        ALU.pow).then_inc(rstd_ready, 1)

            def difference(k, s):
                pool.wait_ge(n_ready, k + 1)
                nc.gpsimd.tensor_tensor(d_sb[s % 2][:, :], hT[s][:, :], n_sb[s % 2][:, :],
                                        ALU.subtract).then_inc(diff_ready, 1)

            def update(k, s):
                pool.wait_ge(zdiff_ready, k + 1)
                nc.gpsimd.tensor_tensor(hT[s][:, :], n_sb[s % 2][:, :], d_sb[s % 2][:, :],
                                        ALU.add).then_inc(h_ready, 1)

            def low(s):
                return nc.gpsimd.tensor_tensor(hT_lo[s][:, :], hT[s][:, :], hT_hi[s][:, :].bitcast(F32), ALU.subtract)

            def take_h0(w, s):
                pool.wait_ge(h0T_hi_ready, w * SLOTS + s + 1)
                low(s).then_inc(h0T_lo_ready, 1)

            def body(kind, w, layer, before, after):
                for s in range(SLOTS):
                    k = item(w, layer, s)
                    prv = (s - 1) % SLOTS
                    has_prev = before or s > 0
                    if has_prev:
                        difference(k - 1, prv)
                    if takes_x(kind, s, after):
                        take_h0(*entering(kind, w, s, after, 1))
                    if not before and s == 0:
                        root(0, 3, 3)
                    if keeps(kind, s):
                        pool.wait_ge(h_hi_ready, kept(w, layer, s) - 1)
                        low((s - 2) % SLOTS).then_inc(h_lo_ready, 1)
                    if has_prev:
                        update(k - 1, prv)
                    if kind != FIRST and after and s == 1:
                        root(w + 1, layer - 1, 0)

            nc.gpsimd.memset(table_in[:, :], 0.0).then_inc(zeroed, 1)
            nc.gpsimd.memset(ident[:, :], 0.0).then_inc(zeroed, 1)
            pool.wait_ge(zeroed, 2)
            nc.gpsimd.affine_select(out=ident[:, :], in_=ident[:, :], compare_op=ALU.not_equal, fill=1.0, base=0,
                                    pattern=[[-1, P]], channel_multiplier=1).then_inc(ident_ready, 1)
            nc.gpsimd.memset(minus_half[:, :], -0.5).then_inc(zeroed, 1)
            pool.wait_ge(zeroed, 3)
            root(0, 0, 0)
            root(0, 1, 1)
            take_h0(0, 0)
            root(0, 2, 2)
            layers(pool, body)


def kernel(x, adj, nodemask, L0_gnn_weight, L0_gnn_w_ih, L0_gnn_w_hh, L0_gnn_b_ih, L0_gnn_b_hh):
    import numpy as np
    import concourse.bacc as bacc
    from concourse.bass_utils import run_bass_kernel_spmd

    lay = np.ascontiguousarray
    x, adj, nodemask = np.asarray(x), np.asarray(adj), np.asarray(nodemask)
    weight, w_ih, w_hh = np.asarray(L0_gnn_weight), np.asarray(L0_gnn_w_ih), np.asarray(L0_gnn_w_hh)
    b_ih, b_hh = np.asarray(L0_gnn_b_ih), np.asarray(L0_gnn_b_hh)
    arrays = {
        "x": lay(x),
        "adj": lay(adj),
        "mask": lay(nodemask.reshape(-1, GRAPHS, P).transpose(0, 2, 1)),
        "weight_t": lay(weight.transpose(2, 0, 1)),
        "w_ih_t": lay(w_ih.T),
        "w_hh_t": lay(w_hh.T),
        "b_ih": lay(b_ih.reshape(GATES, P).T),
        "b_hh": lay(b_hh.reshape(GATES, P).T),
    }
    nc = bacc.Bacc("TRN2", target_bir_lowering=False, num_devices=1)
    args = [nc.dram_tensor(f"in_{n}", a.shape, mybir.dt.from_np(a.dtype), kind="ExternalInput").ap()
            for n, a in arrays.items()]
    out = nc.dram_tensor("out", x.shape, F32, kind="ExternalOutput").ap()
    gnn_kernel(nc, *args, out)
    r = run_bass_kernel_spmd(nc, [{f"in_{n}": a for n, a in arrays.items()}], core_ids=[0])
    return r.results[0]["out"]
```

```python
from contextlib import ExitStack

import concourse.bass as bass
from concourse import mybir

ALU = mybir.AluOpType
ACT = mybir.ActivationFunctionType
F32 = mybir.dt.float32
F32R = mybir.dt.float32r
F16 = mybir.dt.float16

P = 128
GRAPHS = 4
COLS = GRAPHS * P
SLOTS = 4
GATES = 3
EPS = 1e-5
NAT_SCALE = 2.0 ** 11
WARM_UP = 20
DMA = 16

FIRST, MIDDLE, LAST = range(3)


def gnn_kernel(nc, x, adj, mask, weight_t, w_ih_t, w_hh_t, b_ih, b_hh, out):
    B, L = x.shape[0], weight_t.shape[1]
    GROUPS = B // GRAPHS
    WAVES = GROUPS // SLOTS
    ITEMS = L * SLOTS
    V = 2 * GATES * P
    KEPT = (L - 1) * SLOTS
    assert L - 1 == SLOTS
    assert x.shape[1] == P and x.shape[2] == P and GROUPS % SLOTS == 0 and L >= 3 and WAVES >= 2

    x_g = x.rearrange("(g b) n d -> g n b d", b=GRAPHS)
    adj_g = adj.rearrange("(g b) i j -> g i b j", b=GRAPHS)
    out_g = out.rearrange("(g b) n d -> g n b d", b=GRAPHS)

    with ExitStack() as ctx:
        def sb(name, shape, dt=F32):
            return ctx.enter_context(nc.sbuf_tensor(name, shape, dt))

        def bank(name):
            return ctx.enter_context(nc.psum_tensor(name, [P, COLS], F32))

        def sem(name):
            return ctx.enter_context(nc.semaphore(name))

        wt = sb("wt", [P, L, P])
        wih = sb("wih", [P, GATES * P])
        whh = sb("whh", [P, GATES * P])
        whh_hl = sb("whh_hl", [P, V], F32R)
        v_all = sb("v_all", [P, L * V], F32R)
        v_cur = sb("v_cur", [P, V], F32R)
        bih = sb("bih", [P, GATES])
        bhh = sb("bhh", [P, GATES])
        bsum = sb("bsum", [P, GATES])
        ident = sb("ident", [P, P])
        minus_half = sb("minus_half", [P, GRAPHS])
        table_in, table_out = sb("table_in", [P, 1]), sb("table_out", [P, 1])

        x_in = sb("x_in", [P, SLOTS * GRAPHS, P])
        x_res = [sb(f"x_res{s}", [P, GRAPHS, P]) for s in range(SLOTS)]
        mask_s = [sb(f"mask{s}", [P, GRAPHS]) for s in range(SLOTS)]
        adj_in = [sb(f"adj_in{s}", [P, COLS]) for s in range(SLOTS)]
        edges = [sb(f"edges{s}", [P, COLS], F16) for s in range(SLOTS)]
        hT = [sb(f"hT{s}", [P, COLS]) for s in range(SLOTS)]
        hT_hi = [sb(f"hT_hi{s}", [P, COLS], F32R) for s in range(SLOTS)]
        hT_lo = [sb(f"hT_lo{s}", [P, COLS], F32R) for s in range(SLOTS)]
        y = [sb(f"y{s}", [P, GRAPHS, P]) for s in range(SLOTS)]

        def each_slot(name, shape):
            return [sb(f"{name}{s}", shape) for s in range(SLOTS)]

        def pair(name, dt=F32):
            return [sb(f"{name}{i}", [P, COLS], dt) for i in range(2)]

        nat_hi, nat_lo = pair("nat_hi", F16), pair("nat_lo", F16)
        agg_hi, agg_lo = pair("agg_hi", F32R), pair("agg_lo", F32R)
        r_sb, t_sb, n_sb, d_sb = pair("r"), pair("t"), pair("n"), pair("d")

        normed = sb("normed", [P, SLOTS * COLS])
        stats = each_slot("stats", [P, GRAPHS, 6])
        moment = each_slot("moment", [P, GRAPHS, 2])
        var_eps = each_slot("var_eps", [P, GRAPHS])
        rstd = each_slot("rstd", [P, GRAPHS])

        ps_t, ps_agg, ps_out = bank("ps_t"), bank("ps_agg"), bank("ps_out")
        ps_r, ps_hn, ps_in = bank("ps_r"), bank("ps_hn"), bank("ps_in")
        ps_z = [bank("ps_z0"), bank("ps_z1")]
        EARLY_V = 3
        ps_v = [ps_in, ps_hn, ps_z[1], ps_z[1], ps_out]
        assert L == len(ps_v)

        w_loaded, wih_loaded, whh_loaded, b_loaded = sem("w_loaded"), sem("wih_loaded"), sem("whh_loaded"), sem("b_loaded")
        x_loaded = [sem(f"x_loaded{s}") for s in range(SLOTS)]
        adj_loaded = [sem(f"adj_loaded{s}") for s in range(SLOTS)]
        res_loaded = [sem(f"res_loaded{s}") for s in range(SLOTS)]
        stored = [sem(f"stored{s}") for s in range(SLOTS)]
        zeroed, ident_ready, bias_ready = sem("zeroed"), sem("ident_ready"), sem("bias_ready")
        whh_hi_ready, whh_lo_ready = sem("whh_hi_ready"), sem("whh_lo_ready")
        v_done, v_hi_ready, v_lo_ready = sem("v_done"), sem("v_hi_ready"), sem("v_lo_ready")
        t_done, agg_done = sem("t_done"), sem("agg_done")
        r_done, z_done, hn_done, in_done = sem("r_done"), sem("z_done"), sem("hn_done"), sem("in_done")
        nat_hi_ready, nat_lo_ready = sem("nat_hi_ready"), sem("nat_lo_ready")
        agg_hi_ready, agg_lo_ready = sem("agg_hi_ready"), sem("agg_lo_ready")
        r_ready, z_ready, n_ready = sem("r_ready"), sem("z_ready"), sem("n_ready")
        rhn_ready, pre_n_ready = sem("rhn_ready"), sem("pre_n_ready")
        diff_ready, zdiff_ready, h_ready = sem("diff_ready"), sem("zdiff_ready"), sem("h_ready")
        last_diff_ready, last_zdiff_ready, last_h_ready = sem("last_diff_ready"), sem("last_zdiff_ready"), sem("last_h_ready")
        h_hi_ready, h_lo_ready = sem("h_hi_ready"), sem("h_lo_ready")
        v_cur_ready = sem("v_cur_ready")
        stats_ready, moments_ready = sem("stats_ready"), sem("moments_ready")
        var_ready, rstd_ready = sem("var_ready"), sem("rstd_ready")
        normed_ready, edges_ready = sem("normed_ready"), sem("edges_ready")
        h0T_hi_ready, h0T_lo_ready = sem("h0T_hi_ready"), sem("h0T_lo_ready")
        out_done, y_ready = sem("out_done"), sem("y_ready")

        def graph(t, b):
            return t[:, b * P:(b + 1) * P]

        def v_part(layer, part):
            return v_all[:, layer * V + part * V // 2:layer * V + (part + 1) * V // 2]

        def x_slot(s):
            return x_in[:, s * GRAPHS:(s + 1) * GRAPHS, :]

        def normed_slot(s):
            return normed[:, s * COLS:(s + 1) * COLS]

        def graphs(t):
            return t.rearrange("p (b c) -> p b c", b=GRAPHS)

        def item(w, layer, s):
            return w * ITEMS + layer * SLOTS + s

        def keeps(kind, s):
            return {FIRST: s >= 2, MIDDLE: True, LAST: s < 2}[kind]

        def kept(w, layer, s):
            return w * KEPT + layer * SLOTS + s

        def layers(eng, body):
            def rest(w, after):
                with eng.Fori(1, L - 1) as layer:
                    body(MIDDLE, w, layer, True, after)
                body(LAST, w, L - 1, True, after)

            body(FIRST, 0, 0, False, True)
            with eng.Fori(0, WAVES - 1) as w:
                rest(w, True)
                body(FIRST, w + 1, 0, True, True)
            rest(WAVES - 1, False)

        def finished(kind, w, s, ago):
            if kind == LAST and s >= ago:
                return w, s - ago
            if kind == FIRST and s < ago and not (isinstance(w, int) and w == 0):
                return w - 1, s + SLOTS - ago
            return None

        def entering(kind, w, s, after, ahead):
            if kind == FIRST and s + ahead < SLOTS:
                return w, s + ahead
            if kind == LAST and after and 0 <= s + ahead - SLOTS < SLOTS:
                return w + 1, s + ahead - SLOTS
            return None

        def takes_x(kind, s, after):
            return (kind == FIRST and s < SLOTS - 1) or (kind == LAST and s == SLOTS - 1 and after)

        block = ctx.enter_context(nc.Block())

        @block.sync
        def _(sp):
            def load_x(w, s):
                sp.dma_start(x_slot(s), x_g[w * SLOTS + s]).then_inc(x_loaded[s], DMA)

            def load_adj(w, s):
                sp.dma_start(graphs(adj_in[s][:, :]), adj_g[w * SLOTS + s]).then_inc(adj_loaded[s], DMA)

            def load(w):
                for s in range(SLOTS):
                    sp.wait_ge(normed_ready, (w - 1) * SLOTS + s + 1)
                    sp.wait_ge(edges_ready, (w - 1) * SLOTS + s + 1)
                    sp.wait_ge(res_loaded[s], w * 2 * DMA)
                    load_x(w, s)
                    load_adj(w, s)

            def residual(w, s):
                sp.wait_ge(x_loaded[s], (w + 1) * DMA)
                sp.dma_start(x_res[s][:, :, :], x_slot(s)).then_inc(res_loaded[s], DMA)
                sp.dma_start(mask_s[s][:, :], mask[w * SLOTS + s]).then_inc(res_loaded[s], DMA)

            def wave_end(w, after):
                for s in range(SLOTS):
                    sp.wait_ge(y_ready, w * SLOTS + s + 1)
                    sp.dma_start(out_g[w * SLOTS + s], y[s][:, :, :]).then_inc(stored[s], DMA)
                    if after:
                        residual(w + 1, s)

            for s in range(0, SLOTS, 2):
                for do in (load_x, load_adj):
                    do(0, s)
                    do(0, s + 1)
            for s in range(SLOTS):
                residual(0, s)
            load(1)
            with sp.Fori(0, WAVES - 2) as w:
                wave_end(w, True)
                load(w + 2)
            wave_end(WAVES - 2, True)
            wave_end(WAVES - 1, False)
            for s in range(SLOTS):
                sp.wait_ge(stored[s], WAVES * DMA)

        @block.tensor
        def _(pe):
            def aggregate(k, s):
                pe.wait_ge(nat_lo_ready, k + 1)
                for b in range(GRAPHS):
                    for part, nat in enumerate((nat_hi[s % 2], nat_lo[s % 2])):
                        last = nc.tensor.matmul(graph(ps_agg, b), graph(nat, b), graph(edges[s], b),
                                                start=(part == 0), stop=(part == 1))
                last.then_inc(agg_done, 1)

            def product(ps, gate, w_hl, hi, lo, start, stop):
                w_hi, w_lo = w_hl[:, gate * P:(gate + 1) * P], w_hl[:, (GATES + gate) * P:(GATES + gate + 1) * P]
                nc.tensor.matmul(ps[:, :], w_hi, hi[:, :], start=start, stop=False)
                nc.tensor.matmul(ps[:, :], w_lo, hi[:, :], start=False, stop=False)
                return nc.tensor.matmul(ps[:, :], w_hi, lo[:, :], start=False, stop=stop)

            def output(w, s, k_last, bank=ps_out):
                if k_last is not None:
                    pe.wait_ge(h_ready, k_last + 1)
                if bank is ps_out and not (isinstance(w, int) and w == 0 and s == 0):
                    pe.wait_ge(y_ready, w * SLOTS + s)
                for b in range(GRAPHS):
                    last = nc.tensor.transpose(graph(bank, b), graph(hT[s], b), ident[:, :])
                last.then_inc(out_done, 1)

            def body(kind, w, layer, before, after):
                for s in range(SLOTS):
                    k = item(w, layer, s)
                    nxt = (s + 1) % SLOTS
                    has_next = after or kind != LAST or s < SLOTS - 1
                    if has_next:
                        if takes_x(kind, s, after):
                            gw, gs = entering(kind, w, s, after, 1)
                            pe.wait_ge(normed_ready, gw * SLOTS + gs + 1)
                        src = normed_slot(nxt) if takes_x(kind, s, after) else hT[nxt]
                        if not takes_x(kind, s, after):
                            pe.wait_ge(h_ready, k - SLOTS + 2)
                        pe.wait_ge(nat_lo_ready, k + 1)
                        if kind == FIRST:
                            pe.wait_ge(h0T_hi_ready, w * SLOTS + s + 1)
                        for b in range(GRAPHS):
                            last = nc.tensor.transpose(graph(ps_t, b), graph(src, b), ident[:, :])
                        last.then_inc(t_done, 1)

                    if kind == FIRST:
                        pe.wait_ge(h0T_lo_ready, w * SLOTS + s + 1)
                        if not before and s == 0:
                            pe.wait_ge(whh_lo_ready, 1)
                    else:
                        pe.wait_ge(h_lo_ready, kept(w, layer - 1, s + 1))
                    if before or s >= 1:
                        pe.wait_ge(r_ready, k)
                    product(ps_r, 0, whh_hl, hT_hi[s], hT_lo[s], True, False)
                    if before or s >= 2:
                        pe.wait_ge(zdiff_ready, k - 1)
                    elif s == 1:
                        pe.wait_ge(v_lo_ready, 4)
                    product(ps_z[s % 2], 1, whh_hl, hT_hi[s], hT_lo[s], True, False)
                    if before or s >= 1:
                        pe.wait_ge(rhn_ready, k)
                    else:
                        pe.wait_ge(v_lo_ready, ps_v.index(ps_hn) + 1)
                    product(ps_hn, 2, whh_hl, hT_hi[s], hT_lo[s], True, True).then_inc(hn_done, 1)
                    if not before and s == 0:
                        pe.wait_ge(v_lo_ready, 3)
                        v_product(3)

                    if has_next:
                        if takes_x(kind, s, after):
                            gw, gs = entering(kind, w, s, after, 1)
                            pe.wait_ge(edges_ready, gw * SLOTS + gs + 1)
                        pe.wait_ge(agg_lo_ready, k + 1)
                        aggregate(k + 1, nxt)
                    else:
                        pe.wait_ge(agg_lo_ready, k + 1)

                    if kind == MIDDLE:
                        if s == 0:
                            pe.wait_ge(v_cur_ready, w * (L - 2) + layer)
                        v = v_cur
                    else:
                        if s == 0:
                            pe.wait_ge(v_lo_ready, layer + 1)
                        v = v_all[:, layer * V:(layer + 1) * V]
                    ah, al = agg_hi[s % 2], agg_lo[s % 2]
                    product(ps_r, 0, v, ah, al, False, True).then_inc(r_done, 1)
                    product(ps_z[s % 2], 1, v, ah, al, False, True).then_inc(z_done, 1)
                    if before or s >= 1:
                        pe.wait_ge(pre_n_ready, k)
                    product(ps_in, 2, v, ah, al, True, True).then_inc(in_done, 1)

                    if not before and s == 0:
                        v_product(4)
                    group = finished(kind, w, s, 2)
                    if group:
                        output(*group, k - 2)

            def v_product(layer):
                nc.tensor.matmul(ps_v[layer][:, 0:GATES * P], wt[:, layer, :], wih[:, :],
                                 start=True, stop=True).then_inc(v_done, 1)

            pe.wait_ge(ident_ready, 1)
            for i in range(WARM_UP):
                nc.tensor.transpose(graph(ps_t, i % GRAPHS), ident[:, :], ident[:, :])
            pe.wait_ge(w_loaded, DMA)
            pe.wait_ge(wih_loaded, DMA)
            v_product(0)
            pe.wait_ge(normed_ready, 1)
            for b in range(GRAPHS):
                last = nc.tensor.transpose(graph(ps_t, b), graph(normed, b), ident[:, :])
            last.then_inc(t_done, 1)
            for layer in range(1, EARLY_V):
                v_product(layer)
            pe.wait_ge(edges_ready, 1)
            aggregate(0, 0)

            layers(pe, body)
            output(WAVES - 1, SLOTS - 2, item(WAVES - 1, L - 1, SLOTS - 2))
            pe.wait_ge(last_h_ready, 1)
            output(WAVES - 1, SLOTS - 1, None, ps_t)

        @block.scalar
        def _(act):
            def nat_high(k, s, src, function, scale):
                nc.scalar.activation(nat_hi[s % 2][:, :], src, function, scale=scale).then_inc(nat_hi_ready, 1)

            def take_x(w, k, s):
                act.wait_ge(normed_ready, w * SLOTS + s + 1)
                nat_high(k, s, normed_slot(s), ACT.Relu, 1.0)
                act.wait_ge(t_done, k + 1)
                if not (isinstance(w, int) and w == 0):
                    act.wait_ge(out_done, (w - 1) * SLOTS + s + 1)
                nc.scalar.activation(hT[s][:, :], ps_t[:, :], ACT.Relu, scale=1 / NAT_SCALE)
                nc.scalar.activation(hT_hi[s][:, :], ps_t[:, :], ACT.Relu,
                                     scale=1 / NAT_SCALE).then_inc(h0T_hi_ready, 1)

            def agg_high(k, s, free):
                act.wait_ge(agg_done, k + 1)
                if free:
                    act.wait_ge(in_done, k - 1)
                nc.scalar.copy(agg_hi[s % 2][:, :], ps_agg[:, :]).then_inc(agg_hi_ready, 1)

            def tanh(k, s, free):
                act.wait_ge(pre_n_ready, k + 1)
                if free:
                    act.wait_ge(h_ready, k - 1)
                nc.scalar.activation(n_sb[s % 2][:, :], t_sb[s % 2][:, :], ACT.Tanh,
                                     bias=bih[:, 2:3]).then_inc(n_ready, 1)

            def body(kind, w, layer, before, after):
                for s in range(SLOTS):
                    k = item(w, layer, s)
                    nxt, prv, ago2 = (s + 1) % SLOTS, (s - 1) % SLOTS, (s - 2) % SLOTS
                    has_prev, has_next = before or s > 0, after or kind != LAST or s < SLOTS - 1
                    if kind == MIDDLE and s == 0:
                        act.wait_ge(v_lo_ready, L)
                        act.wait_ge(in_done, k)
                        nc.scalar.copy(v_cur[:, :], v_all[:, bass.ds(layer * V, V)]).then_inc(v_cur_ready, 1)
                    if has_next and takes_x(kind, s, after):
                        gw, gs = entering(kind, w, s, after, 1)
                        act.wait_ge(agg_done, k)
                        take_x(gw, k + 1, gs)
                    elif has_next:
                        act.wait_ge(t_done, k + 2)
                        act.wait_ge(agg_done, k)
                        nat_high(k + 1, nxt, ps_t[:, :], ACT.Copy, NAT_SCALE)
                    if has_prev:
                        tanh(k - 1, prv, before or s >= 3)
                    if keeps(kind, s):
                        act.wait_ge(h_ready, k - 1)
                        nc.scalar.copy(hT_hi[ago2][:, :], hT[ago2][:, :]).then_inc(h_hi_ready, 1)
                    if has_next:
                        agg_high(k + 1, nxt, has_prev)
                    if not before and s == 0:
                        v_high(3)
                    act.wait_ge(r_done, k + 1)
                    if before or s >= 2:
                        act.wait_ge(rhn_ready, k - 1)
                    nc.scalar.activation(r_sb[s % 2][:, :], ps_r[:, :], ACT.Sigmoid,
                                         bias=bsum[:, 0:1]).then_inc(r_ready, 1)
                    act.wait_ge(z_done, k + 1)
                    nc.scalar.activation(ps_z[s % 2][:, :], ps_z[s % 2][:, :], ACT.Sigmoid,
                                         bias=bsum[:, 1:2]).then_inc(z_ready, 1)
                    if not before and s == 0:
                        v_high(4)

            act.dma_start(wih[:, :], w_ih_t).then_inc(wih_loaded, DMA)
            act.dma_start(wt[:, :, :], weight_t).then_inc(w_loaded, DMA)
            act.dma_start(whh[:, :], w_hh_t).then_inc(whh_loaded, DMA)
            act.dma_start(bih[:, :], b_ih).then_inc(b_loaded, DMA)
            act.dma_start(bhh[:, :], b_hh).then_inc(b_loaded, DMA)
            act.wait_ge(zeroed, 1)
            nc.scalar.activation(table_out[:, :], table_in[:, :], ACT.Sigmoid)

            def v_high(layer):
                act.wait_ge(v_done, layer + 1)
                nc.scalar.mul(v_part(layer, 0), ps_v[layer][:, 0:GATES * P], 1 / NAT_SCALE).then_inc(v_hi_ready, 1)

            act.wait_ge(whh_loaded, DMA)
            nc.scalar.copy(whh_hl[:, 0:V // 2], whh[:, :]).then_inc(whh_hi_ready, 1)
            v_high(0)
            take_x(0, 0, 0)
            for layer in range(1, EARLY_V):
                v_high(layer)
            agg_high(0, 0, False)
            act.wait_ge(bias_ready, 1)
            layers(act, body)
            tanh(WAVES * ITEMS - 1, SLOTS - 1, True)

        @block.vector
        def _(dve):
            def edge_matrix(w, s):
                dve.wait_ge(adj_loaded[s], (w + 1) * DMA)
                if not (isinstance(w, int) and w == 0):
                    dve.wait_ge(agg_done, item(w - 1, L - 1, s) + 1)
                nc.vector.tensor_scalar(edges[s][:, :], adj_in[s][:, :], 0.0, None,
                                        ALU.not_equal).then_inc(edges_ready, 1)

            def statistics(w, s, i):
                for slot in (s,) if isinstance(s, int) else range(SLOTS):
                    dve.wait_ge(x_loaded[slot], (w + 1) * DMA)
                for b in range(GRAPHS):
                    last = nc.vector.bn_stats(stats[i][:, b, :], x_graph(s, b))
                last.then_inc(stats_ready, 1)

            def moments(i):
                for b in range(GRAPHS):
                    last = nc.vector.bn_aggr(moment[i][:, b, :], stats[i][:, b, :])
                last.then_inc(moments_ready, 1)

            def normalise(w, s, i, of=range(GRAPHS)):
                dve.wait_ge(rstd_ready, w * SLOTS + s + 1)
                for b in of:
                    last = nc.vector.tensor_scalar(normed[:, bass.ds(s * COLS + b * P, P)], x_graph(s, b),
                                                   moment[i][:, b, 0:1], rstd[i][:, b:b + 1], ALU.subtract, ALU.mult)
                if of[-1] == GRAPHS - 1:
                    last.then_inc(normed_ready, 1)

            def x_graph(s, b):
                return x_flat[:, bass.ds(s * COLS + b * P, P)]

            x_flat = x_in[:, :, :].rearrange("p g c -> p (g c)")

            def nat_low(k, s, src, op, scalar):
                dve.wait_ge(nat_hi_ready, k + 1)
                nc.vector.scalar_tensor_tensor(out=nat_lo[s % 2][:, :], in0=src, scalar=scalar,
                                               in1=nat_hi[s % 2][:, :], op0=op,
                                               op1=ALU.subtract).then_inc(nat_lo_ready, 1)

            def agg_low(k, s, free):
                dve.wait_ge(agg_hi_ready, k + 1)
                if free:
                    dve.wait_ge(in_done, k - 1)
                nc.vector.tensor_tensor(agg_lo[s % 2][:, :], ps_agg[:, :], agg_hi[s % 2][:, :].bitcast(F32),
                                        ALU.subtract).then_inc(agg_lo_ready, 1)

            def pre_n(k, s):
                dve.wait_ge(in_done, k + 1)
                dve.wait_ge(rhn_ready, k + 1)
                nc.vector.tensor_tensor(t_sb[s % 2][:, :], ps_in[:, :], t_sb[s % 2][:, :],
                                        ALU.add).then_inc(pre_n_ready, 1)

            def zdiff(k, s):
                dve.wait_ge(diff_ready, k + 1)
                dve.wait_ge(z_ready, k + 1)
                nc.vector.tensor_tensor(d_sb[s % 2][:, :], ps_z[s % 2][:, :], d_sb[s % 2][:, :],
                                        ALU.mult).then_inc(zdiff_ready, 1)

            def output(w, s, bank=ps_out):
                g = w * SLOTS + s
                dve.wait_ge(out_done, g + 1)
                dve.wait_ge(res_loaded[s], (w + 1) * 2 * DMA)
                if not (isinstance(w, int) and w == 0):
                    dve.wait_ge(stored[s], w * DMA)
                for b in range(GRAPHS):
                    last = nc.vector.scalar_tensor_tensor(out=y[s][:, b, :], in0=graph(bank, b),
                                                          scalar=mask_s[s][:, b:b + 1], in1=x_res[s][:, b, :],
                                                          op0=ALU.mult, op1=ALU.add)
                last.then_inc(y_ready, 1)

            def body(kind, w, layer, before, after):
                for s in range(SLOTS):
                    k = item(w, layer, s)
                    nxt, prv = (s + 1) % SLOTS, (s - 1) % SLOTS
                    has_prev, has_next = before or s > 0, after or kind != LAST or s < SLOTS - 1
                    group = (w + 1, layer - 1, 0) if kind != FIRST and after else None
                    if group and s == 1:
                        dve.wait_ge(stats_ready, (w + 1) * SLOTS + layer)
                    if has_prev:
                        pre_n(k - 1, prv)
                    if takes_x(kind, s, after):
                        nat_low(k + 1, nxt, normed_slot(nxt), ALU.max, 0.0)
                    elif has_next:
                        nat_low(k + 1, nxt, ps_t[:, :], ALU.mult, NAT_SCALE)
                    if group and s >= 2:
                        normalise(*group, (0, 1) if s == 2 else (2, 3))
                    if not before and s == 0:
                        statistics(0, 2, 2)
                    leaving, coming = finished(kind, w, s, 3), entering(kind, w, s, after, 2)
                    if coming:
                        edge_matrix(*coming)
                    if leaving:
                        output(*leaving)
                    if not before and s == 0:
                        dve.wait_ge(stats_ready, 3)
                        moments(2)
                    if not before and s == 1:
                        normalise(0, 3, 3)
                    if not before and s == 1:
                        v_low(4)
                    if group and s == 0:
                        statistics(*group)
                    if group and s == 1:
                        moments(0)
                    if has_next:
                        agg_low(k + 1, nxt, has_prev)
                    if has_prev:
                        zdiff(k - 1, prv)
                    if not before and s == 0:
                        statistics(0, 3, 3)
                        normalise(0, 2, 2)
                        v_low(3)
                    dve.wait_ge(r_ready, k + 1)
                    dve.wait_ge(hn_done, k + 1)
                    if before or s >= 2:
                        dve.wait_ge(n_ready, k - 1)
                    nc.vector.scalar_tensor_tensor(out=t_sb[s % 2][:, :], in0=ps_hn[:, :], scalar=bhh[:, 2:3],
                                                   in1=r_sb[s % 2][:, :], op0=ALU.add,
                                                   op1=ALU.mult).then_inc(rhn_ready, 1)
                    if not before and s == 0:
                        dve.wait_ge(stats_ready, 4)
                        moments(3)

            def v_low(layer):
                dve.wait_ge(v_hi_ready, layer + 1)
                nc.vector.scalar_tensor_tensor(out=v_part(layer, 1), in0=ps_v[layer][:, 0:GATES * P],
                                               scalar=1 / NAT_SCALE, in1=v_part(layer, 0).bitcast(F32),
                                               op0=ALU.mult, op1=ALU.subtract).then_inc(v_lo_ready, 1)

            for s in range(2):
                statistics(0, s, s)
                dve.wait_ge(stats_ready, s + 1)
                moments(s)
            normalise(0, 0, 0)
            edge_matrix(0, 0)
            nat_low(0, 0, normed_slot(0), ALU.max, 0.0)
            normalise(0, 1, 1)
            dve.wait_ge(b_loaded, 2 * DMA)
            nc.vector.tensor_tensor(bsum[:, :], bih[:, :], bhh[:, :], ALU.add).then_inc(bias_ready, 1)
            for layer in range(EARLY_V):
                v_low(layer)
            edge_matrix(0, 1)
            agg_low(0, 0, False)
            layers(dve, body)
            k, s = WAVES * ITEMS - 1, SLOTS - 1
            pre_n(k, s)
            output(WAVES - 1, s - 2)
            dve.wait_ge(n_ready, k + 1)
            nc.vector.tensor_tensor(d_sb[s % 2][:, :], hT[s][:, :], n_sb[s % 2][:, :],
                                    ALU.subtract).then_inc(last_diff_ready, 1)
            dve.wait_ge(last_diff_ready, 1)
            dve.wait_ge(z_ready, k + 1)
            nc.vector.tensor_tensor(d_sb[s % 2][:, :], ps_z[s % 2][:, :], d_sb[s % 2][:, :],
                                    ALU.mult).then_inc(last_zdiff_ready, 1)
            dve.wait_ge(last_zdiff_ready, 1)
            nc.vector.tensor_tensor(hT[s][:, :], n_sb[s % 2][:, :], d_sb[s % 2][:, :],
                                    ALU.add).then_inc(last_h_ready, 1)
            output(WAVES - 1, s - 1)
            output(WAVES - 1, s, ps_t)

        @block.gpsimd
        def _(pool):
            def root(w, s, i):
                nc.gpsimd.tensor_scalar(var_eps[i][:, :], moment[i][:, :, 1], 1 / NAT_SCALE ** 2, EPS / NAT_SCALE ** 2,
                                        ALU.mult, ALU.add).then_inc(var_ready, 1)
                pool.wait_ge(var_ready, w * SLOTS + s + 1)
                nc.gpsimd.tensor_tensor(rstd[i][:, :], var_eps[i][:, :], minus_half[:, :],
                                        ALU.pow).then_inc(rstd_ready, 1)

            def difference(k, s):
                pool.wait_ge(n_ready, k + 1)
                nc.gpsimd.tensor_tensor(d_sb[s % 2][:, :], hT[s][:, :], n_sb[s % 2][:, :],
                                        ALU.subtract).then_inc(diff_ready, 1)

            def update(k, s):
                pool.wait_ge(zdiff_ready, k + 1)
                nc.gpsimd.tensor_tensor(hT[s][:, :], n_sb[s % 2][:, :], d_sb[s % 2][:, :],
                                        ALU.add).then_inc(h_ready, 1)

            def low(s):
                return nc.gpsimd.tensor_tensor(hT_lo[s][:, :], hT[s][:, :], hT_hi[s][:, :].bitcast(F32), ALU.subtract)

            def take_h0(w, s):
                pool.wait_ge(h0T_hi_ready, w * SLOTS + s + 1)
                low(s).then_inc(h0T_lo_ready, 1)

            def body(kind, w, layer, before, after):
                for s in range(SLOTS):
                    k = item(w, layer, s)
                    prv = (s - 1) % SLOTS
                    has_prev = before or s > 0
                    if has_prev:
                        difference(k - 1, prv)
                    if takes_x(kind, s, after):
                        take_h0(*entering(kind, w, s, after, 1))
                    if not before and s == 0:
                        for other in (2, 3):
                            pool.wait_ge(moments_ready, other + 1)
                            root(0, other, other)
                    if keeps(kind, s):
                        pool.wait_ge(h_hi_ready, kept(w, layer, s) - 1)
                        low((s - 2) % SLOTS).then_inc(h_lo_ready, 1)
                    if kind != FIRST and after and s == 1:
                        pool.wait_ge(moments_ready, (w + 1) * SLOTS + layer)
                    if has_prev:
                        update(k - 1, prv)
                    if kind != FIRST and after and s == 1:
                        root(w + 1, layer - 1, 0)

            nc.gpsimd.memset(table_in[:, :], 0.0).then_inc(zeroed, 1)
            nc.gpsimd.memset(ident[:, :], 0.0).then_inc(zeroed, 1)
            pool.wait_ge(zeroed, 2)
            nc.gpsimd.affine_select(out=ident[:, :], in_=ident[:, :], compare_op=ALU.not_equal, fill=1.0, base=0,
                                    pattern=[[-1, P]], channel_multiplier=1).then_inc(ident_ready, 1)
            nc.gpsimd.memset(minus_half[:, :], -0.5).then_inc(zeroed, 1)
            pool.wait_ge(zeroed, 3)
            for s in range(2):
                pool.wait_ge(moments_ready, s + 1)
                root(0, s, s)
            pool.wait_ge(whh_hi_ready, 1)
            nc.gpsimd.tensor_tensor(whh_hl[:, V // 2:V], whh[:, :], whh_hl[:, 0:V // 2].bitcast(F32),
                                    ALU.subtract).then_inc(whh_lo_ready, 1)
            take_h0(0, 0)
            layers(pool, body)


def kernel(x, adj, nodemask, L0_gnn_weight, L0_gnn_w_ih, L0_gnn_w_hh, L0_gnn_b_ih, L0_gnn_b_hh):
    import numpy as np
    import concourse.bacc as bacc
    from concourse.bass_utils import run_bass_kernel_spmd

    lay = np.ascontiguousarray
    x, adj, nodemask = np.asarray(x), np.asarray(adj), np.asarray(nodemask)
    weight, w_ih, w_hh = np.asarray(L0_gnn_weight), np.asarray(L0_gnn_w_ih), np.asarray(L0_gnn_w_hh)
    b_ih, b_hh = np.asarray(L0_gnn_b_ih), np.asarray(L0_gnn_b_hh)
    arrays = {
        "x": lay(x),
        "adj": lay(adj),
        "mask": lay(nodemask.reshape(-1, GRAPHS, P).transpose(0, 2, 1)),
        "weight_t": lay(weight.transpose(2, 0, 1)),
        "w_ih_t": lay(w_ih.T),
        "w_hh_t": lay(w_hh.T),
        "b_ih": lay(b_ih.reshape(GATES, P).T),
        "b_hh": lay(b_hh.reshape(GATES, P).T),
    }
    nc = bacc.Bacc("TRN2", target_bir_lowering=False, num_devices=1)
    args = [nc.dram_tensor(f"in_{n}", a.shape, mybir.dt.from_np(a.dtype), kind="ExternalInput").ap()
            for n, a in arrays.items()]
    out = nc.dram_tensor("out", x.shape, F32, kind="ExternalOutput").ap()
    gnn_kernel(nc, *args, out)
    r = run_bass_kernel_spmd(nc, [{f"in_{n}": a for n, a in arrays.items()}], core_ids=[0])
    return r.results[0]["out"]
```
